# Optimizing a Trainium2 kernel written in Bass

```python
import numpy as np
import jax
import jax.numpy as jnp

def _softmax(x, axis=-1):
    return jax.nn.softmax(x, axis=axis)

def _gelu(x):
    return jax.nn.gelu(x, approximate=True)

def _silu(x):
    return jax.nn.silu(x)

def _sigmoid(x):
    return jax.nn.sigmoid(x)

def _layernorm(x, axis=-1, eps=1e-05):
    m = jnp.mean(x, axis=axis, keepdims=True)
    v = jnp.var(x, axis=axis, keepdims=True)
    return (x - m) / jnp.sqrt(v + eps)

def _scatter_add(tgt, idx, src, axis=0):
    return tgt.at[idx].add(src)

def _segment_sum(src, seg, n):
    return jax.ops.segment_sum(src, seg, n)
kernel_name = 'mk_seq_preln_d1_jaxref_r8_3473b1'

def setup_inputs(seed: int=0):
    np.random.seed(seed)
    _w = jnp.asarray

    def _L0_attn_setup():
        import jax, jax.numpy as jnp
        import numpy as np
        EPS = 1e-12
        HEADS = 16
        DIM_KEYS = 16
        DIM_VALUES = 64

        def l2norm(t):
            n = jnp.linalg.norm(t, axis=-1, keepdims=True)
            return t / jnp.maximum(n, EPS)

        def tanh_norm(t):
            n = jnp.linalg.norm(t, axis=-1, keepdims=True)
            return jnp.tanh(n) * (t / jnp.maximum(n, EPS))

        def split_heads(x, h):
            b, n, hd = x.shape
            return x.reshape(b, n, h, hd // h).transpose(0, 2, 1, 3)
        key = jax.random.key(seed)
        k1, k2, k3, k4 = jax.random.split(key, 4)
        b, n, dim = (4, 256, 128)
        dim_inner = (DIM_KEYS + DIM_VALUES) * HEADS
        tokens = jax.random.normal(k1, (b, n, dim), dtype=jnp.float32)
        Wqg = jax.random.normal(k2, (dim, dim_inner), dtype=jnp.float32) * dim ** (-0.5)
        Wkv = jax.random.normal(k3, (dim, dim_inner), dtype=jnp.float32) * dim ** (-0.5)
        Wout = jax.random.normal(k4, (DIM_VALUES * HEADS, dim), dtype=jnp.float32) * (DIM_VALUES * HEADS) ** (-0.5)
        return {'tokens': tokens, 'Wqg': Wqg, 'Wkv': Wkv, 'Wout': Wout}
    _L0_attn_in = _L0_attn_setup()

    def _L0_ffn_setup():
        import jax, jax.numpy as jnp
        import numpy as np
        H = 128
        M = 64
        E = 16
        TOP_K = 4
        N_GROUP = 4
        TOPK_GROUP = 2
        SCALE = 2.5
        B, S = (2, 128)

        def _gate(x2d, gate_kernel, gate_bias):
            n = x2d.shape[0]
            logits = jnp.dot(x2d.astype(jnp.float32), gate_kernel.astype(jnp.float32))
            scores = jax.nn.sigmoid(logits)
            scores_for_choice = scores + gate_bias
            group_scores = scores_for_choice.reshape(n, N_GROUP, E // N_GROUP)
            top2 = jax.lax.top_k(group_scores, k=2)[0]
            group_sum = jnp.sum(top2, axis=-1)
            group_idx = jax.lax.top_k(group_sum, k=TOPK_GROUP)[1]
            group_mask = jnp.zeros_like(group_sum).at[jnp.arange(n)[:, None], group_idx].set(1.0)
            score_mask = jnp.repeat(group_mask[:, :, None], E // N_GROUP, axis=2).reshape(n, E)
            masked_scores = jnp.where(score_mask > 0, scores_for_choice, 0.0)
            topk_weight, topk_idx = jax.lax.top_k(masked_scores, k=TOP_K)
            topk_weight = topk_weight / (jnp.sum(topk_weight, axis=-1, keepdims=True) + 1e-20)
            topk_weight = topk_weight * SCALE
            return (topk_idx, topk_weight)
        key = jax.random.key(seed)
        ks = jax.random.split(key, 9)
        sc_h = 1.0 / np.sqrt(H)
        sc_m = 1.0 / np.sqrt(M)
        return {'hidden_states': jax.random.normal(ks[0], (B, S, H), jnp.float32), 'gate_kernel': jax.random.normal(ks[1], (H, E), jnp.float32) * sc_h, 'gate_bias': jax.random.normal(ks[2], (E,), jnp.float32) * 0.01, 'w_gate': jax.random.normal(ks[3], (E, H, M), jnp.float32) * sc_h, 'w_up': jax.random.normal(ks[4], (E, H, M), jnp.float32) * sc_h, 'w_down': jax.random.normal(ks[5], (E, M, H), jnp.float32) * sc_m, 'sw_gate': jax.random.normal(ks[6], (H, 2 * M), jnp.float32) * sc_h, 'sw_up': jax.random.normal(ks[7], (H, 2 * M), jnp.float32) * sc_h, 'sw_down': jax.random.normal(ks[8], (2 * M, H), jnp.float32) * (1.0 / np.sqrt(2 * M))}
    _L0_ffn_in = _L0_ffn_setup()
    _d = {'L0_attn_tokens': _L0_attn_in['tokens'], 'L0_attn_Wqg': _L0_attn_in['Wqg'], 'L0_attn_Wkv': _L0_attn_in['Wkv'], 'L0_attn_Wout': _L0_attn_in['Wout'], 'L0_ffn_gate_kernel': _L0_ffn_in['gate_kernel'], 'L0_ffn_gate_bias': _L0_ffn_in['gate_bias'], 'L0_ffn_w_gate': _L0_ffn_in['w_gate'], 'L0_ffn_w_up': _L0_ffn_in['w_up'], 'L0_ffn_w_down': _L0_ffn_in['w_down'], 'L0_ffn_sw_gate': _L0_ffn_in['sw_gate'], 'L0_ffn_sw_up': _L0_ffn_in['sw_up'], 'L0_ffn_sw_down': _L0_ffn_in['sw_down']}
    _x0 = _d['L0_attn_tokens']
    _d['L0_attn_tokens'] = jax.random.normal(jax.random.fold_in(jax.random.key(seed), 1), (16, 256, 128), dtype=_x0.dtype)
    del _x0
    return _d

def reference(L0_attn_tokens, L0_attn_Wqg, L0_attn_Wkv, L0_attn_Wout, L0_ffn_gate_kernel, L0_ffn_gate_bias, L0_ffn_w_gate, L0_ffn_w_up, L0_ffn_w_down, L0_ffn_sw_gate, L0_ffn_sw_up, L0_ffn_sw_down):

    def _L0_attn_ref(tokens, Wqg, Wkv, Wout):
        import jax, jax.numpy as jnp
        import numpy as np
        EPS = 1e-12
        HEADS = 16
        DIM_KEYS = 16
        DIM_VALUES = 64

        def l2norm(t):
            n = jnp.linalg.norm(t, axis=-1, keepdims=True)
            return t / jnp.maximum(n, EPS)

        def tanh_norm(t):
            n = jnp.linalg.norm(t, axis=-1, keepdims=True)
            return jnp.tanh(n) * (t / jnp.maximum(n, EPS))

        def split_heads(x, h):
            b, n, hd = x.shape
            return x.reshape(b, n, h, hd // h).transpose(0, 2, 1, 3)
        qg = split_heads(tokens @ Wqg, HEADS)
        kv = split_heads(tokens @ Wkv, HEADS)
        queries, gates = (qg[..., :DIM_KEYS], qg[..., DIM_KEYS:])
        keys, values = (kv[..., :DIM_KEYS], kv[..., DIM_KEYS:])
        queries, keys, values = (l2norm(queries), l2norm(keys), l2norm(values))
        sim = jnp.einsum('bhid,bhjd->bhij', queries, keys)
        attn = jnp.square(jax.nn.relu(sim))
        aggr = jnp.einsum('bhij,bhjd->bhid', attn, values)
        out = tanh_norm(aggr) * jnp.tanh(jax.nn.silu(gates))
        b, h, n, d = out.shape
        out = out.transpose(0, 2, 1, 3).reshape(b, n, h * d)
        return out @ Wout

    def _L0_ffn_ref(hidden_states, gate_kernel, gate_bias, w_gate, w_up, w_down, sw_gate, sw_up, sw_down):
        import jax, jax.numpy as jnp
        import numpy as np
        H = 128
        M = 64
        E = 16
        TOP_K = 4
        N_GROUP = 4
        TOPK_GROUP = 2
        SCALE = 2.5
        B, S = (2, 128)

        def _gate(x2d, gate_kernel, gate_bias):
            n = x2d.shape[0]
            logits = jnp.dot(x2d.astype(jnp.float32), gate_kernel.astype(jnp.float32))
            scores = jax.nn.sigmoid(logits)
            scores_for_choice = scores + gate_bias
            group_scores = scores_for_choice.reshape(n, N_GROUP, E // N_GROUP)
            top2 = jax.lax.top_k(group_scores, k=2)[0]
            group_sum = jnp.sum(top2, axis=-1)
            group_idx = jax.lax.top_k(group_sum, k=TOPK_GROUP)[1]
            group_mask = jnp.zeros_like(group_sum).at[jnp.arange(n)[:, None], group_idx].set(1.0)
            score_mask = jnp.repeat(group_mask[:, :, None], E // N_GROUP, axis=2).reshape(n, E)
            masked_scores = jnp.where(score_mask > 0, scores_for_choice, 0.0)
            topk_weight, topk_idx = jax.lax.top_k(masked_scores, k=TOP_K)
            topk_weight = topk_weight / (jnp.sum(topk_weight, axis=-1, keepdims=True) + 1e-20)
            topk_weight = topk_weight * SCALE
            return (topk_idx, topk_weight)
        orig_shape = hidden_states.shape
        x = hidden_states.reshape(-1, orig_shape[-1])
        topk_idx, topk_weight = _gate(x, gate_kernel, gate_bias)
        onehot = (topk_idx[:, :, None] == jnp.arange(E)[None, None, :]).astype(topk_weight.dtype)
        combine = jnp.einsum('nke,nk->ne', onehot, topk_weight)
        g = jnp.einsum('nh,ehm->enm', x, w_gate)
        u = jnp.einsum('nh,ehm->enm', x, w_up)
        inter = jax.nn.silu(g) * u
        y_e = jnp.einsum('enm,emh->enh', inter, w_down)
        y = jnp.einsum('ne,enh->nh', combine, y_e)
        shared = jnp.dot(jax.nn.silu(jnp.dot(x, sw_gate)) * jnp.dot(x, sw_up), sw_down)
        return (y + shared).reshape(orig_shape)
    x = L0_attn_tokens
    x = x + _L0_attn_ref(_layernorm(x, axis=-1), L0_attn_Wqg, L0_attn_Wkv, L0_attn_Wout)
    x = x + _L0_ffn_ref(_layernorm(x, axis=-1), L0_ffn_gate_kernel, L0_ffn_gate_bias, L0_ffn_w_gate, L0_ffn_w_up, L0_ffn_w_down, L0_ffn_sw_gate, L0_ffn_sw_up, L0_ffn_sw_down)
    return x

_drawn_inputs = setup_inputs


def setup_inputs(seed=0):
    import zlib

    import numpy as np

    out = dict(_drawn_inputs(seed))
    spreads = {}
    factors = {}
    for name, (base, spread) in spreads.items():
        noise = np.random.default_rng([zlib.crc32(name.encode()), seed]).standard_normal(out[name].shape)
        drawn = base * np.exp(spread * noise) if base else spread * noise
        out[name] = jnp.asarray(drawn.astype(out[name].dtype))
    for name, factor in factors.items():
        out[name] = (out[name] * factor).astype(out[name].dtype)
    return out
```

```python
from contextlib import ExitStack

import concourse.bass as bass
from concourse import mybir

F32 = mybir.dt.float32
F32R = mybir.dt.float32r
I32 = mybir.dt.int32
ALU = mybir.AluOpType
ACT = mybir.ActivationFunctionType
AX = mybir.AxisListType

P = 128
EPS_LN = 1e-5
TINY = 1e-35
INV_EPS = 1e12
RSQRT_MAGIC = 1597463007.0
SCALE = 2.5
REPLACED = -3.0e38
SENTINEL = -2.0e38


def bass_attn_moe_layer_kernel(nc, tokens, Wqg, Wkv, Wout, gate_kernel, gate_bias,
                               w_gate, w_up, w_down, sw_gate, sw_up, sw_down, out):
    B, N, D = tokens.shape
    E, _, M = w_gate.shape
    T = N // P
    DV = 64
    H = Wout.shape[0] // DV
    DK = Wqg.shape[1] // H - DV
    NP = H // 2
    EC = E // 2
    FC = EC + 1
    NG = 4
    EG = E // NG
    TOP_K = 4
    HK = H * DK
    HV = H * DV
    SLOTS = NP
    assert D == P and T == 2 and DK == 16 and 2 * M == P and 2 * DV == P and H == E == 16 and FC == 9

    FILL = [
        [("P", "qk", 0), ("P", "qk", 1), ("P", "v", 0), ("O", "ones", 0)],
        [("P", "v", 1), ("P", "v", 2), ("O", "nT", 0), ("P", "v", 3)],
        [("P", "g", 0), ("P", "g", 1), ("O", "rT", 0), ("P", "g", 2)],
        [("P", "g", 3), ("O", "rB", 0), ("O", "rB", 1), ("O", "rB", 2), ("O", "rB", 3)],
        [("O", "y", 0), ("P", "tr", 0), ("P", "tr", 1), ("P", "tr", 2)],
        [("P", "tr", 3), ("P", "tr", 4), ("P", "tr", 5), ("P", "tr", 6), ("P", "tr", 7), ("F", "x2T", 0)],
        [("F", "lg", 0)] + [("F", "gu", c) for c in range(4)],
        [("F", "gu", c) for c in range(4, FC)] + [("F", "cT", 0), ("L", "xT", 0)]
        + [("F", "cB", j) for j in range(4)] + [("F", "y2", 0)],
    ]
    ORDER = [job for slot in FILL for job in slot]
    assert len(FILL) == SLOTS and len(ORDER) % 4 == 0
    OFFSET = {"L": 2, "P": 1, "A": 0, "O": -1, "F": -1}
    JOBS = {"xT": 1, "qk": 2, "v": 4, "g": 4, "tr": NP, "ones": 1, "nT": 1, "rT": 1, "rB": 4, "y": 1,
            "x2T": 1, "lg": 1, "gu": FC, "cT": 1, "cB": 4, "y2": 1}

    def stages(s):
        return {k for k, d in OFFSET.items() if 0 <= s + d < B}

    ALL = set(OFFSET)
    FIRST_STEP, LOOP_FROM, LOOP_TO, LAST_STEP = -2, 2, B - 2, B
    assert all(stages(s) == ALL for s in range(1, LOOP_TO)) and (LOOP_TO - LOOP_FROM) % 2 == 0

    with ExitStack() as ctx:
        def sb(name, shape, dt=F32):
            return ctx.enter_context(nc.sbuf_tensor(name, shape, dt))

        def sem(name):
            return ctx.enter_context(nc.semaphore(name))

        wqk = [sb(f"wqk_{k}", [P, 2 * HK], F32R) for k in ("hi", "lo")]
        wv = [sb(f"wv_{k}", [P, HV], F32R) for k in ("hi", "lo")]
        wg = [sb(f"wg_{k}", [P, HV], F32R) for k in ("hi", "lo")]
        weg = [sb(f"weg_{k}", [P, FC * P], F32R) for k in ("hi", "lo")]
        weu = [sb(f"weu_{k}", [P, FC * P], F32R) for k in ("hi", "lo")]
        wout = sb("wout", [P, NP, D])
        wdown = sb("wdown", [P, FC, D])
        wroute = sb("wroute", [P, E])
        bias = sb("bias", [P, E])
        ident = sb("ident", [P, P])
        ones16 = sb("ones16", [P, NP, H])
        sel = sb("sel", [2 * H, NP, P], F32R)
        lower = sb("lower", [P, NG, NG])
        RAW = 2 * (HK + HV) + 2 * FC * P
        big = sb("big", [P, max(RAW, 3 * NP * N)])
        aw = [big[:, q * NP * N:(q + 1) * NP * N].rearrange("p (c n) -> p c n", n=N) for q in range(2)]
        a2 = big[:, 2 * NP * N:3 * NP * N].rearrange("p (c n) -> p c n", n=N)
        x_in = [sb(f"x_in{q}", [P, T, D]) for q in range(2)]
        x_res = [sb(f"x_res{q}", [P, T, D]) for q in range(2)]
        xn = sb("xn", [P, T, D])
        xh, xl = sb("xh", [P, N], F32R), sb("xl", [P, N], F32R)
        qk = sb("qk", [P, T, 2 * HK])
        qks = sb("qks", [P, T, 2 * H, 4, DK], F32R)
        qkt = [sb(f"qkt{q}", [P, NP, 2 * N], F32R) for q in range(2)]
        v = [sb(f"v{q}", [P, T, HV]) for q in range(2)]
        wt = [sb(f"wt{q}", [P, NP, N]) for q in range(2)]
        r = [sb(f"r{k}", [P, 2 * N]) for k in range(2)]
        p = [sb(f"p{k}", [P, 2 * N]) for k in range(4)]
        rs = sb("rs", [P, T, 2, H])
        rt = sb("rt", [2 * H, N], F32R)
        og = sb("og", [P, NP, N])
        sqq = og[:, 0:4, :].rearrange("p (t c) n -> p t (c n)", t=T)
        sqv = og[:, 4:8, :].rearrange("p c n -> p (c n)")
        selraw = og[0:2 * H, 0:4, :].rearrange("p c (e n) -> p (c e) n", e=2)
        x1 = sb("x1", [P, T, D])
        n2row = x1[0:H].rearrange("p t d -> p (t d)")
        x2h, x2l = sb("x2h", [P, N], F32R), sb("x2l", [P, N], F32R)
        sg = [sb(f"sg{k}", [P, N]) for k in range(2)]
        it = sb("it", [P, FC, N])
        cs = sb("cs", [P, T, 2, E])
        o_sb = sb("o_sb", [P, T, D])

        def norm_tiles(name, n):
            return {k: sb(f"{name}_{k}", [P, n]) for k in ("m", "y", "t")}

        st1, mv1, nt1 = sb("st1", [P, T, 6]), sb("mv1", [P, T, 2]), norm_tiles("ln1", T)
        st2, mv2, nt2 = sb("st2", [P, T, 6]), sb("mv2", [P, T, 2]), norm_tiles("ln2", T)
        S3 = 2 * H + H
        ss, ntp = sb("ss", [P, T, S3]), norm_tiles("qkv", T * S3)
        n2, nn, tn, nto = sb("n2", [P, T * H]), sb("nn", [P, T * H]), sb("tn", [P, T * H]), norm_tiles("an", T * H)
        rr = sb("rr", [P, T * H])
        th, sc = sb("th", [P, T * E]), sb("sc", [P, T * E])
        pairs, gsum = sb("pairs", [P, T * NG, 6]), sb("gsum", [P, T * NG])
        gt, eq = sb("gt", [P, T, NG, NG]), sb("eq", [P, T, NG, NG])
        rank = sb("rank", [P, T * NG])
        masked = sb("masked", [P, T * NG, EG])
        EB = E + 8
        cand, repl = sb("cand", [P, T, EB]), sb("repl", [P, T, EB])
        top = sb("top", [P, T, 8])
        chosen = sb("chosen", [P, T, E])
        den, comb = sb("den", [P, T]), sb("comb", [P, T, E])
        split_hi = sb("split_hi", [P, T, H], F32R)
        carrier = sb("carrier", [P, 1])

        ps_s = [ctx.enter_context(nc.psum_tensor(f"ps_s{k}", [P, 512], F32)) for k in range(2)]
        ps_a = [ctx.enter_context(nc.psum_tensor(f"ps_a{k}", [P, 512], F32)) for k in range(2)]
        ps_f = [ctx.enter_context(nc.psum_tensor(f"ps_f{k}", [P, 512], F32)) for k in range(4)]
        bank = {job[1:]: ps_f[n % 4] for n, job in enumerate(ORDER)}

        x_loaded = [sem(f"x_loaded{q}") for q in range(2)]
        w_loaded = [sem(f"w_loaded{k}") for k in range(3)]
        c_loaded = sem("c_loaded")
        out_stored = sem("out_stored")
        consts_pool, consts_dve = sem("consts_pool"), sem("consts_dve")
        w_hi, w_lo = sem("w_hi"), sem("w_lo")
        done = {k: sem(f"{k}_done") for k in JOBS}
        read = {k: sem(f"{k}_read") for k in JOBS}
        scores_done, values_done = sem("scores_done"), sem("values_done")
        relu_done, probs_done = sem("relu_done"), sem("probs_done")
        a2_done, aw_done = sem("a2_done"), sem("aw_done")
        ln1_ready, xh_ready, x_kept = sem("ln1_ready"), sem("xh_ready"), sem("x_kept")
        sqq_done, sqv_done, sums_done = sem("sqq_done"), sem("sqv_done"), sem("sums_done")
        qk_normed, v_normed = sem("qk_normed"), sem("v_normed")
        qk_hi, qk_lo = sem("qk_hi"), sem("qk_lo")
        gate_ready = sem("gate_ready")
        n_ready, tanh_n, r_ready = sem("n_ready"), sem("tanh_n"), sem("r_ready")
        ln2_ready, x2h_ready = sem("ln2_ready"), sem("x2h_ready")
        silu_done, c_ready = sem("silu_done"), sem("c_ready")
        ch_l, ch_p, ch_o, ch_f = sem("ch_l"), sem("ch_p"), sem("ch_o"), sem("ch_f")

        block = ctx.enter_context(nc.Block())

        def run_steps(eng, step):
            for s in range(FIRST_STEP, LOOP_FROM):
                step(s, s % 2, stages(s), s)
            with eng.Fori(LOOP_FROM // 2, LOOP_TO // 2) as i:
                step(i * 2, 0, ALL, None)
                step(i * 2 + 1, 1, ALL, None)
            for s in range(LOOP_TO, LAST_STEP + 1):
                step(s, s % 2, stages(s), s)

        def wait(eng, semaphore, value):
            if not isinstance(value, int) or value > 0:
                eng.wait_ge(semaphore, value)

        def broadcast(ap, shape, at):
            return ap.unsqueeze(at).broadcast_to(shape)

        def slots_of(part, t):
            heads = qks[:, t, H * part:H * part + H, :, :]
            if part == 0:
                heads = heads.rearrange("p h (r a) d -> p a h r d", a=2)
            else:
                heads = heads.rearrange("p h (a r) d -> p a h r d", a=2)
            whole = qk[:, t, HK * part:HK * part + HK].rearrange("p (h d) -> p h d", d=DK)
            return heads[:, 0], heads[:, 1], broadcast(whole, [P, H, 2, DK], 2)

        @block.sync
        def _(sp):
            def load_x(b, q):
                sp.dma_start(x_in[q][:], tokens[b].rearrange("(t p) d -> p t d", p=P)).then_inc(x_loaded[q], 16)

            load_x(0, 0)
            sp.dma_start(big[:, 0:HK + HV], Wqg).then_inc(w_loaded[0], 16)
            sp.dma_start(big[:, HK + HV:2 * (HK + HV)], Wkv).then_inc(w_loaded[0], 16)
            load_x(1, 1)
            base = 2 * (HK + HV)
            for w, sw in ((w_gate, sw_gate), (w_up, sw_up)):
                k = 1 if w is w_gate else 2
                sp.dma_start(big[:, base:base + E * M].rearrange("p (e m) -> p e m", m=M),
                             w.rearrange("e h m -> h e m")).then_inc(w_loaded[k], 16)
                sp.dma_start(big[:, base + E * M:base + FC * P], sw).then_inc(w_loaded[k], 16)
                base += FC * P
            sp.dma_start(wout[:], Wout.rearrange("(c p) n -> p c n", p=P)).then_inc(c_loaded, 16)
            sp.dma_start(wdown[:, 0:EC, :], w_down.rearrange("(c e) m h -> (e m) c h", e=2)).then_inc(c_loaded, 16)
            sp.dma_start(wdown[:, EC, :], sw_down).then_inc(c_loaded, 16)
            sp.dma_start(wroute[:], gate_kernel).then_inc(c_loaded, 16)
            sp.dma_start(bias[:], gate_bias.rearrange("(a e) -> a e", a=1).broadcast_to([P, E])).then_inc(c_loaded, 16)

            def step(s, q, on, at):
                if "L" in on and "A" in on:
                    sp.wait_ge(x_kept, s + 1)
                    sp.wait_ge(ln1_ready, s + 1)
                    load_x(s + 2, q)
                if "F" in on:
                    sp.wait_ge(read["y2"], s)
                    sp.dma_start(out[s - 1].rearrange("(t p) d -> p t d", p=P), o_sb[:])\
                      .then_inc(out_stored, 16)

            run_steps(sp, step)
            sp.wait_ge(out_stored, 16 * B)

        @block.gpsimd
        def _(pool):
            n = [0]

            def built(ins):
                n[0] += 1
                ins.then_inc(consts_pool, 1)
                pool.wait_ge(consts_pool, n[0])

            built(pool.memset(ident[:], 0.0))
            built(pool.affine_select(out=ident[:], in_=ident[:], compare_op=ALU.not_equal, fill=1.0, base=0,
                                     pattern=[[-1, P]], channel_multiplier=1))
            built(pool.memset(selraw, 0.0))
            for part in range(2):
                view = selraw.rearrange("k c (e m) -> k c e m", e=2)
                built(pool.affine_select(out=view, in_=view, compare_op=ALU.not_equal, fill=1.0, base=-H * part,
                                         pattern=[[-2, NP], [-1, 2], [0, DV]], channel_multiplier=1))

            def step(s, q, on, at):
                for k in range(SLOTS):
                    if "A" in on:
                        for h in (2 * k, 2 * k + 1):
                            wait(pool, values_done, 8 * s + (h - 4) // 2 + 1)
                            pool.wait_ge(relu_done, 16 * s + h + 1)
                            pool.tensor_tensor(p[h % 4][:], r[h % 2][:], r[h % 2][:], ALU.mult).then_inc(probs_done, 1)
                    if "P" in on:
                        b = s + 1
                        if k == 0:
                            wait(pool, sums_done, 4 * b)
                            wait(pool, done["y"], b - 2)
                            for t in range(T):
                                pool.wait_ge(read["qk"], 2 * b + t + 1)
                                pool.tensor_tensor(sqq[:, t, :], qk[:, t, :], qk[:, t, :], ALU.mult)\
                                    .then_inc(sqq_done, 1)
                        if k in (1, 2):
                            t = k - 1
                            if t == 1:
                                pool.wait_ge(sums_done, 4 * b + 3)
                            pool.wait_ge(read["v"], 4 * b + 2 * t + 2)
                            pool.tensor_tensor(sqv, v[1 - q][:, t, :], v[1 - q][:, t, :], ALU.mult)\
                                .then_inc(sqv_done, 1)
                        if k == 3:
                            wait(pool, done["tr"], 8 * b)
                            for t in range(T):
                                for part in range(2):
                                    pool.wait_ge(qk_hi, 4 * b + 2 * t + part + 1)
                                    hi, lo, whole = slots_of(part, t)
                                    pool.tensor_tensor(lo, whole, hi.bitcast(F32), ALU.subtract).then_inc(qk_lo, 1)

            run_steps(pool, step)

        @block.tensor
        def _(pe):
            pe.wait_ge(consts_pool, 5)
            pe.wait_ge(consts_dve, 2)
            pe.wait_ge(w_lo, 7)

            def three(dst, stat, mov):
                pe.matmul(dst, stat[0], mov[0], start=True, stop=False)
                pe.matmul(dst, stat[0], mov[1], start=False, stop=False)
                return pe.matmul(dst, stat[1], mov[0], start=False, stop=True)

            def filler(stage, kind, j, s, q):
                b = s + OFFSET[stage]
                ps = bank[(kind, j)]
                pb = 1 - q
                tok = [slice(t * P, (t + 1) * P) for t in range(T)]
                if kind == "xT":
                    pe.wait_ge(ln1_ready, b + 1)
                    for t in range(T):
                        last = pe.transpose(ps[:, tok[t]], xn[:, t, :], ident[:])
                elif kind == "qk":
                    if j == 0:
                        pe.wait_ge(xh_ready, b + 1)
                        pe.wait_ge(read["xT"], b + 1)
                    last = three(ps[:, 0:2 * HK], (xh[:, tok[j]], xl[:, tok[j]]), (wqk[0][:], wqk[1][:]))
                elif kind == "v":
                    half = slice((j % 2) * 512, (j % 2 + 1) * 512)
                    last = three(ps[:, :], (xh[:, tok[j // 2]], xl[:, tok[j // 2]]), (wv[0][:, half], wv[1][:, half]))
                elif kind == "g":
                    for c in range(2):
                        cols = slice((2 * j + c) * P, (2 * j + c + 1) * P)
                        last = three(ps[:, c * N:(c + 1) * N], (wg[0][:, cols], wg[1][:, cols]), (xh[:], xl[:]))
                elif kind == "tr":
                    if j == 0:
                        pe.wait_ge(qk_lo, 4 * b + 4)
                    for part in range(2):
                        for t in range(T):
                            src = qks[:, t, H * part + 2 * j:H * part + 2 * j + 2, :, :].bitcast(F32)
                            src = src.rearrange("p h a d -> p (h a d)")
                            last = pe.transpose(ps[:, part * N + t * P:part * N + (t + 1) * P], src, ident[:])
                elif kind == "ones":
                    pe.wait_ge(a2_done, 8 * b + 8)
                    for c in range(NP):
                        last = pe.matmul(ps[0:H, 0:N], ones16[:, c, :], a2[:, c, :], start=(c == 0), stop=(c == NP - 1))
                elif kind == "nT":
                    pe.wait_ge(read["ones"], b + 1)
                    for t in range(T):
                        last = pe.matmul(ps[:, t * H:(t + 1) * H], n2row[:, tok[t]], ident[0:H, 0:H],
                                         start=True, stop=True)
                elif kind in ("rT", "cT"):
                    pe.wait_ge(r_ready if kind == "rT" else c_ready, b + 1)
                    src = rs if kind == "rT" else cs
                    for t in range(T):
                        last = pe.transpose(ps[0:2 * H, tok[t]], src[:, t, :, :].rearrange("p a h -> p (a h)"), ident[:])
                elif kind in ("rB", "cB"):
                    ready = read["rT" if kind == "rB" else "cT"]
                    if j == 0:
                        pe.wait_ge(ready, b + 1)
                    for c in range(2):
                        last = pe.matmul(ps[:, c * N:(c + 1) * N], sel[:, 2 * j + c, :], rt[:], start=True, stop=True)
                elif kind == "y":
                    pe.wait_ge(read["rB"], 4 * b + 4)
                    for t in range(T):
                        for c in range(NP):
                            last = pe.matmul(ps[:, tok[t]], og[:, c, tok[t]], wout[:, c, :],
                                             start=(c == 0), stop=(c == NP - 1))
                elif kind == "x2T":
                    pe.wait_ge(ln2_ready, b + 1)
                    for t in range(T):
                        last = pe.transpose(ps[:, tok[t]], xn[:, t, :], ident[:])
                elif kind == "lg":
                    pe.wait_ge(x2h_ready, b + 1)
                    pe.wait_ge(read["x2T"], b + 1)
                    for t in range(T):
                        pe.matmul(ps[:, t * E:(t + 1) * E], x2h[:, tok[t]].bitcast(F32), wroute[:], start=True, stop=False)
                        last = pe.matmul(ps[:, t * E:(t + 1) * E], x2l[:, tok[t]].bitcast(F32), wroute[:],
                                         start=False, stop=True)
                elif kind == "gu":
                    cols = slice(j * P, (j + 1) * P)
                    three(ps[:, 0:N], (weg[0][:, cols], weg[1][:, cols]), (x2h[:], x2l[:]))
                    last = three(ps[:, N:2 * N], (weu[0][:, cols], weu[1][:, cols]), (x2h[:], x2l[:]))
                else:
                    pe.wait_ge(read["cB"], 4 * b + 4)
                    for t in range(T):
                        for c in range(FC):
                            last = pe.matmul(ps[:, tok[t]], it[:, c, tok[t]], wdown[:, c, :],
                                             start=(c == 0), stop=(c == FC - 1))
                last.then_inc(done[kind], 1)

            def wait_for_bank(n, s, at):
                m, d = n - 4, 0
                while True:
                    if m < 0:
                        m, d = m + len(ORDER), d - 1
                    stage, kind, j = ORDER[m]
                    if at is None or stage in stages(at + d):
                        break
                    if at + d < FIRST_STEP:
                        return
                    m -= 4
                wait(pe, read[kind], (s + d + OFFSET[stage]) * JOBS[kind] + j + 1)

            def step(s, q, on, at):
                n = 0
                for k in range(SLOTS):
                    if "A" in on:
                        for e in range(2):
                            h = 2 * k + e
                            if h == 0:
                                pe.wait_ge(read["tr"], 8 * s + 8)
                            wait(pe, relu_done, 16 * s + h - 1)
                            rows = slice(64 * e, 64 * e + 64)
                            for t in range(T):
                                last = pe.matmul(ps_s[e][:, t * N:(t + 1) * N],
                                                 qkt[q][rows, k, N + t * P:N + (t + 1) * P], qkt[q][rows, k, 0:N],
                                                 start=True, stop=True)
                            last.then_inc(scores_done, 1)
                    for stage, kind, j in FILL[k]:
                        if stage in on:
                            wait_for_bank(n, s, at)
                            filler(stage, kind, j, s, q)
                        n += 1
                    if "A" in on:
                        wait(pe, aw_done, 8 * s + k - 1)
                        if k == 0:
                            pe.wait_ge(v_normed, s + 1)
                        for t in range(T):
                            for e in range(2):
                                h = 2 * k + e
                                if t == 0:
                                    pe.wait_ge(probs_done, 16 * s + h + 1)
                                last = pe.matmul(ps_a[k % 2][64 * e:64 * e + 64, 0:N],
                                                 v[q][:, t, h * DV:(h + 1) * DV], p[h % 4][:, t * N:(t + 1) * N],
                                                 start=(t == 0), stop=(t == T - 1))
                        last.then_inc(values_done, 1)

            run_steps(pe, step)

        @block.scalar
        def _(act):
            act.wait_ge(w_loaded[0], 32)
            gq = big[:, 0:HK + HV].rearrange("p (h c) -> p h c", h=H)
            kv = big[:, HK + HV:2 * (HK + HV)].rearrange("p (h c) -> p h c", h=H)
            base = 2 * (HK + HV)

            def heads(w, c):
                return w.rearrange("p (h c) -> p h c", c=c)

            act.activation(heads(wqk[0][:, 0:HK], DK), gq[:, :, 0:DK], ACT.Copy).then_inc(w_hi, 1)
            act.activation(heads(wqk[0][:, HK:2 * HK], DK), kv[:, :, 0:DK], ACT.Copy).then_inc(w_hi, 1)
            act.activation(heads(wv[0][:], DV), kv[:, :, DK:], ACT.Copy).then_inc(w_hi, 1)
            act.activation(heads(wg[0][:], DV), gq[:, :, DK:], ACT.Copy).then_inc(w_hi, 1)
            act.wait_ge(w_loaded[1], 32)
            act.activation(weg[0][:], big[:, base:base + FC * P], ACT.Copy).then_inc(w_hi, 1)
            act.wait_ge(w_loaded[2], 32)
            act.activation(weu[0][:], big[:, base + FC * P:base + 2 * FC * P], ACT.Copy).then_inc(w_hi, 1)

            def evacuate(stage, kind, j, s, q):
                b = s + OFFSET[stage]
                pq = 1 - q
                ps = bank[(kind, j)]
                count = b * JOBS[kind] + j + 1
                if kind == "xT":
                    wait(act, done["g"], 4 * b)
                    act.wait_ge(done[kind], count)
                    act.activation(xh[:], ps[:, 0:N], ACT.Copy).then_inc(xh_ready, 1)
                elif kind == "qk":
                    wait(act, qk_lo, 4 * b)
                    act.wait_ge(done[kind], count)
                    act.activation(qk[:, j, :], ps[:, 0:2 * HK], ACT.Copy).then_inc(read[kind], 1)
                elif kind == "v":
                    if j == 0:
                        wait(act, values_done, 8 * (b - 1))
                    act.wait_ge(done[kind], count)
                    act.activation(v[pq][:, j // 2, (j % 2) * 512:(j % 2 + 1) * 512], ps[:], ACT.Copy)\
                       .then_inc(read[kind], 1)
                elif kind == "g":
                    if j == 0:
                        wait(act, aw_done, 8 * (b - 1))
                    act.wait_ge(done[kind], count)
                    dst = wt[pq][:, 2 * j:2 * j + 2, :]
                    act.activation(dst, ps[:].rearrange("p (c n) -> p c n", n=N), ACT.Silu).then_inc(read[kind], 1)
                    act.wait_ge(read[kind], count)
                    act.activation(dst, dst, ACT.Tanh).then_inc(gate_ready, 1)
                elif kind == "tr":
                    if j == 0:
                        wait(act, scores_done, 16 * (b - 1))
                    act.wait_ge(done[kind], count)
                    act.activation(qkt[pq][:, j, :], ps[:], ACT.Copy).then_inc(read[kind], 1)
                elif kind in ("rT", "cT"):
                    if kind == "rT":
                        wait(act, done["cB"], 4 * b)
                    else:
                        act.wait_ge(done["rB"], 4 * b + 4)
                    act.wait_ge(done[kind], count)
                    act.activation(rt[:], ps[0:2 * H, 0:N], ACT.Copy).then_inc(read[kind], 1)
                elif kind == "x2T":
                    wait(act, done["gu"], FC * b)
                    act.wait_ge(done[kind], count)
                    act.activation(x2h[:], ps[:, 0:N], ACT.Copy).then_inc(x2h_ready, 1)
                elif kind == "lg":
                    act.wait_ge(done[kind], count)
                    act.activation(th[:], ps[:, 0:T * E], ACT.Tanh, scale=0.5).then_inc(read[kind], 1)
                elif kind == "gu":
                    wait(act, read["gu"], FC * b + j - 1)
                    act.wait_ge(done[kind], count)
                    act.activation(sg[j % 2][:], ps[:, 0:N], ACT.Silu).then_inc(silu_done, 1)

            def step(s, q, on, at):
                for k in range(SLOTS):
                    if "A" in on:
                        for h in (2 * k, 2 * k + 1):
                            wait(act, probs_done, 16 * s + h - 1)
                            act.wait_ge(scores_done, 16 * s + h + 1)
                            act.activation(r[h % 2][:], ps_s[h % 2][:], ACT.Relu).then_inc(relu_done, 1)
                    if ("A" in on and k > 0) or ("O" in on and k == 0):
                        pair, b = (k - 1, s) if k > 0 else (NP - 1, s - 1)
                        if pair == 0:
                            wait(act, done["ones"], s)
                        act.wait_ge(values_done, 8 * b + pair + 1)
                        act.activation(a2[:, pair, :], ps_a[pair % 2][:, 0:N], ACT.Square).then_inc(a2_done, 1)
                    if k == 2 and "O" in on:
                        act.wait_ge(n_ready, s)
                        act.activation(tn[:], nn[:], ACT.Tanh).then_inc(tanh_n, 1)
                    for stage, kind, j in FILL[k]:
                        if stage in on:
                            evacuate(stage, kind, j, s, q)
                    if k == 3 and "P" in on:
                        b = s + 1
                        wait(act, done["tr"], 8 * b)
                        act.wait_ge(qk_normed, b + 1)
                        for t in range(T):
                            for part in range(2):
                                hi, _, whole = slots_of(part, t)
                                act.activation(hi, whole, ACT.Copy).then_inc(qk_hi, 1)

            run_steps(act, step)

        @block.vector
        def _(dve):
            class Chain:

                def __init__(self, semaphore, per, b):
                    self.semaphore, self.per, self.b, self.n = semaphore, per, b, 0

                def __call__(self, ins, apart=False):
                    self.n += 1
                    assert self.n <= self.per
                    ins.then_inc(self.semaphore, 1)
                    dve.wait_ge(self.semaphore, self.b * self.per + self.n)
                    if apart:
                        dve.memset(carrier[:], 0.0)

                def end(self):
                    assert self.n == self.per, self.n

            def rsqrt(link, tiles):
                m, y, t = tiles["m"][:], tiles["y"][:], tiles["t"][:]
                link(dve.tensor_single_scalar(y.bitcast(I32), m.bitcast(I32), 1, ALU.logical_shift_right))
                link(dve.tensor_scalar(y.bitcast(I32), y.bitcast(I32), -1.0, RSQRT_MAGIC, ALU.mult, ALU.add))
                for _ in range(3):
                    link(dve.tensor_tensor(t, y, y, ALU.mult))
                    link(dve.scalar_tensor_tensor(out=t, in0=t, scalar=-0.5, in1=m, op0=ALU.mult, op1=ALU.mult))
                    link(dve.scalar_tensor_tensor(out=y, in0=t, scalar=1.5, in1=y, op0=ALU.add, op1=ALU.mult))

            RS_OPS = 11
            LN_OPS = 3 + RS_OPS
            P_OPS, O_OPS, F_OPS = RS_OPS + 2, RS_OPS + 4, LN_OPS + 21

            def layer_norm(link, x, st, mv, tiles, dst, ready, other, other_count):
                for t in range(T):
                    last = dve.bn_stats(st[:, t, :], x[:, t, :])
                link(last, apart=True)
                for t in range(T):
                    last = dve.bn_aggr(mv[:, t, :], st[:, t, :])
                link(last)
                link(dve.tensor_scalar(tiles["m"][:], mv[:, :, 1], EPS_LN, None, ALU.add))
                rsqrt(link, tiles)
                wait(dve, done[other], other_count)
                for t in range(T):
                    last = dve.tensor_scalar(dst[:, t, :], x[:, t, :], mv[:, t, 0:1], tiles["y"][:, t:t + 1],
                                             ALU.subtract, ALU.mult)
                last.then_inc(ready, 1)

            n = [0]

            def built(ins):
                n[0] += 1
                ins.then_inc(consts_dve, 1)
                dve.wait_ge(consts_dve, n[0])

            dve.wait_ge(consts_pool, 5)
            dve.tensor_copy(sel[:], selraw)
            dve.memset(ones16[:], 0.0)
            dve.memset(lower[:], 0.0)
            built(dve.memset(cand[:], SENTINEL))
            flat = ones16[:].rearrange("p c h -> p (c h)")
            for e in range(2):
                for c in range(NP):
                    dve.memset(ones16[64 * e:64 * e + 64, c, 2 * c + e:2 * c + e + 1], 1.0)
            for g in range(1, NG):
                last = dve.memset(lower[:, g, 0:g], 1.0)
            built(last)

            gq = big[:, 0:HK + HV].rearrange("p (h c) -> p h c", h=H)
            kv = big[:, HK + HV:2 * (HK + HV)].rearrange("p (h c) -> p h c", h=H)
            base = 2 * (HK + HV)

            def rest(k, w, raw, c):
                dve.wait_ge(w_hi, k)
                lo, hi = w[1], w[0]
                if c:
                    lo, hi = lo.rearrange("p (h c) -> p h c", c=c), hi.rearrange("p (h c) -> p h c", c=c)
                dve.tensor_tensor(lo, raw, hi.bitcast(F32), ALU.subtract).then_inc(w_lo, 1)

            rest(1, [w[:, 0:HK] for w in wqk], gq[:, :, 0:DK], DK)
            rest(2, [w[:, HK:2 * HK] for w in wqk], kv[:, :, 0:DK], DK)
            rest(3, [w[:] for w in wv], kv[:, :, DK:], DV)
            rest(4, [w[:] for w in wg], gq[:, :, DK:], DV)
            rest(5, [w[:] for w in weg], big[:, base:base + FC * P], 0)
            rest(6, [w[:] for w in weu], big[:, base + FC * P:base + 2 * FC * P], 0)
            dve.wait_ge(c_loaded, 80)
            dve.tensor_copy(th[:, 0:E], bias[:]).then_inc(w_lo, 1)

            def sums(kind, t, b):
                if kind == "qk":
                    dve.wait_ge(sqq_done, 2 * b + t + 1)
                    dve.tensor_reduce(ss[:, t, 0:2 * H], sqq[:, t, :].rearrange("p (h d) -> p h d", d=DK), AX.X, ALU.add)\
                       .then_inc(sums_done, 1)
                else:
                    dve.wait_ge(sqv_done, 2 * b + t + 1)
                    dve.tensor_reduce(ss[:, t, 2 * H:S3], sqv.rearrange("p (h d) -> p h d", d=DV), AX.X, ALU.add)\
                       .then_inc(sums_done, 1)

            def norm_qkv(b, pq):
                link = Chain(ch_p, P_OPS, b)
                dve.wait_ge(sums_done, 4 * b + 4)
                link(dve.tensor_scalar(ntp["m"][:], ss[:].rearrange("p t h -> p (t h)"), TINY, None, ALU.max))
                rsqrt(link, ntp)
                link(dve.tensor_scalar(ntp["y"][:], ntp["y"][:], INV_EPS, None, ALU.min))
                link.end()
                rn = ntp["y"][:].rearrange("p (t h) -> p t h", t=T)
                for t in range(T):
                    view = qk[:, t, :].rearrange("p (h d) -> p h d", d=DK)
                    last = dve.tensor_tensor(view, view, broadcast(rn[:, t, 0:2 * H], [P, 2 * H, DK], 2), ALU.mult)
                last.then_inc(qk_normed, 1)
                for t in range(T):
                    view = v[pq][:, t, :].rearrange("p (h d) -> p h d", d=DV)
                    last = dve.tensor_tensor(view, view, broadcast(rn[:, t, 2 * H:S3], [P, H, DV], 2), ALU.mult)
                last.then_inc(v_normed, 1)

            def head_norms(link, b):
                dve.wait_ge(done["nT"], b + 1)
                dve.tensor_copy(n2[:], bank[("nT", 0)][:, 0:T * H]).then_inc(read["nT"], 1)
                dve.wait_ge(read["nT"], b + 1)
                link(dve.tensor_scalar(nto["m"][:], n2[:], TINY, None, ALU.max))
                rsqrt(link, nto)
                dve.tensor_tensor(nn[:], n2[:], nto["y"][:], ALU.mult).then_inc(n_ready, 1)
                link(dve.tensor_scalar(nto["y"][:], nto["y"][:], INV_EPS, None, ALU.min))

            def head_scales(link, b):
                dve.wait_ge(tanh_n, b + 1)
                link(dve.tensor_tensor(rr[:], tn[:], nto["y"][:], ALU.mult))
                split(link, rs, rr[:].rearrange("p (t h) -> p t h", t=T), r_ready)

            def split(link, dst, src, ready):
                link(dve.tensor_copy(split_hi[:], src))
                dve.tensor_copy(dst[:, :, 0, :], split_hi[:].bitcast(F32))
                dve.tensor_tensor(dst[:, :, 1, :], src, split_hi[:].bitcast(F32), ALU.subtract).then_inc(ready, 1)

            def route(link, b):
                dve.wait_ge(read["lg"], b + 1)
                link(dve.tensor_scalar(sc[:], th[:], 0.5, 0.5, ALU.mult, ALU.add))
                link(dve.tensor_tensor(sc[:].rearrange("p (t e) -> p t e", t=T), sc[:].rearrange("p (t e) -> p t e", t=T),
                                       broadcast(bias[:], [P, T, E], 1), ALU.add))
                s4 = sc[:].rearrange("p (g e) -> p g e", e=EG)
                dve.tensor_tensor(pairs[:, :, 0:3], s4[:, :, 0:3], s4[:, :, 1:4], ALU.add)
                dve.tensor_tensor(pairs[:, :, 3:5], s4[:, :, 0:2], s4[:, :, 2:4], ALU.add)
                link(dve.tensor_tensor(pairs[:, :, 5:6], s4[:, :, 0:1], s4[:, :, 3:4], ALU.add))
                link(dve.tensor_reduce(gsum[:], pairs[:], AX.X, ALU.max))
                gs = gsum[:].rearrange("p (t g) -> p t g", t=T)
                other, own = broadcast(gs, [P, T, NG, NG], 2), broadcast(gs, [P, T, NG, NG], 3)
                dve.tensor_tensor(gt[:], other, own, ALU.is_gt)
                link(dve.tensor_tensor(eq[:], other, own, ALU.is_equal))
                link(dve.tensor_tensor(eq[:], eq[:], broadcast(lower[:], [P, T, NG, NG], 1), ALU.mult))
                link(dve.tensor_tensor(gt[:], gt[:], eq[:], ALU.add))
                link(dve.tensor_reduce(rank[:].rearrange("p (t g) -> p t g", t=T), gt[:], AX.X, ALU.add))
                link(dve.tensor_scalar(rank[:], rank[:], 2.0, None, ALU.is_lt))
                link(dve.tensor_tensor(masked[:], s4, broadcast(rank[:], [P, T * NG, EG], 2), ALU.mult))
                link(dve.tensor_scalar(cand[:, :, 0:E], masked[:].rearrange("p (t g) e -> p t (g e)", t=T), 0.0, None,
                                       ALU.add), apart=True)
                for t in range(T):
                    last = dve.max(top[:, t, :], cand[:, t, :])
                link(last)
                link(dve.memset(top[:, :, TOP_K:8], SENTINEL), apart=True)
                for t in range(T):
                    last = dve.match_replace(repl[:, t, :], top[:, t, :], cand[:, t, :], REPLACED)
                link(last)
                link(dve.tensor_tensor(chosen[:], repl[:, :, 0:E], cand[:, :, 0:E], ALU.not_equal))
                link(dve.tensor_tensor(chosen[:], chosen[:], cand[:, :, 0:E], ALU.mult))
                link(dve.tensor_reduce(den[:], chosen[:], AX.X, ALU.add))
                link(dve.tensor_scalar(den[:], den[:], 1e-20, None, ALU.add))
                link(dve.reciprocal(den[:], den[:]))
                link(dve.scalar_tensor_tensor(out=comb[:], in0=chosen[:], scalar=SCALE,
                                              in1=broadcast(den[:], [P, T, E], 2), op0=ALU.mult, op1=ALU.mult))
                split(link, cs, comb[:], c_ready)

            def step(s, q, on, at):
                pq = 1 - q
                O = "O" in on
                b = s - 1
                if O:
                    link_o, link_f = Chain(ch_o, O_OPS, b), Chain(ch_f, F_OPS, b)
                for k in range(SLOTS):
                    if ("A" in on and k > 0) or (O and k == 0):
                        pair, ab, ap = (k - 1, s, q) if k > 0 else (NP - 1, b, pq)
                        dve.wait_ge(a2_done, 8 * ab + pair + 1)
                        dve.wait_ge(gate_ready, 4 * ab + pair // 2 + 1)
                        dve.tensor_tensor(aw[ap][:, pair, :], ps_a[pair % 2][:, 0:N], wt[ap][:, pair, :], ALU.mult)\
                           .then_inc(aw_done, 1)
                    if k == 0 and O:
                        dve.wait_ge(done["ones"], b + 1)
                        wait(dve, done["nT"], b)
                        dve.tensor_copy(n2row, bank[("ones", 0)][0:H, 0:N]).then_inc(read["ones"], 1)
                    if k == 1:
                        if "P" in on:
                            for t in range(T):
                                sums("qk", t, s + 1)
                            sums("v", 0, s + 1)
                        if O:
                            head_norms(link_o, b)
                    if k == 2:
                        if O:
                            head_scales(link_o, b)
                            link_o.end()
                        if "P" in on:
                            sums("v", 1, s + 1)
                            norm_qkv(s + 1, pq)
                    if k == 3 and O:
                        for j in range(4):
                            dve.wait_ge(done["rB"], 4 * b + j + 1)
                            if j == 0:
                                wait(dve, done["y"], b)
                                dve.wait_ge(aw_done, 8 * b + 8)
                            dve.tensor_tensor(og[:, 2 * j:2 * j + 2, :],
                                              bank[("rB", j)][:].rearrange("p (c n) -> p c n", n=N),
                                              aw[pq][:, 2 * j:2 * j + 2, :], ALU.mult)\
                               .then_inc(read["rB"], 1)
                    if k == 4 and O:
                        dve.wait_ge(done["y"], b + 1)
                        dve.wait_ge(x_kept, b + 1)
                        wait(dve, read["y2"], b)
                        dve.tensor_tensor(x1[:], bank[("y", 0)][:, 0:N].rearrange("p (t d) -> p t d", d=D),
                                          x_res[pq][:], ALU.add).then_inc(read["y"], 1)
                        dve.wait_ge(read["y"], b + 1)
                        layer_norm(link_f, x1, st2, mv2, nt2, xn, ln2_ready, "xT", min(s + 2, B) if at is not None else s + 2)
                    if k == 5:
                        if "P" in on:
                            wait(dve, read["y"], s)
                            dve.wait_ge(x_loaded[pq], 8 * (s + 1 - pq) + 16)
                            dve.tensor_copy(x_res[pq][:], x_in[pq][:]).then_inc(x_kept, 1)
                        if "L" in on:
                            lb = s + 2
                            link_l = Chain(ch_l, LN_OPS, lb)
                            dve.wait_ge(x_loaded[q], 8 * (lb - q) + 16)
                            layer_norm(link_l, x_in[q], st1, mv1, nt1, xn, ln1_ready, "x2T", s)
                            link_l.end()
                        if O:
                            dve.wait_ge(x2h_ready, b + 1)
                            dve.tensor_tensor(x2l[:], bank[("x2T", 0)][:, 0:N], x2h[:].bitcast(F32), ALU.subtract)\
                               .then_inc(read["x2T"], 1)
                    if k == 6 and O:
                        route(link_f, b)
                        link_f.end()
                    if k in (6, 7) and O:
                        for c in range(*((0, 4) if k == 6 else (4, FC))):
                            dve.wait_ge(silu_done, FC * b + c + 1)
                            if c == 0:
                                wait(dve, done["y2"], b)
                            dve.tensor_tensor(it[:, c, :], bank[("gu", c)][:, N:2 * N], sg[c % 2][:], ALU.mult)\
                               .then_inc(read["gu"], 1)
                    if k == 7:
                        if "L" in on:
                            dve.wait_ge(xh_ready, s + 3)
                            dve.tensor_tensor(xl[:], bank[("xT", 0)][:, 0:N], xh[:].bitcast(F32), ALU.subtract)\
                               .then_inc(read["xT"], 1)
                        if O:
                            dve.wait_ge(read["gu"], FC * b + FC)
                            for j in range(4):
                                dve.wait_ge(done["cB"], 4 * b + j + 1)
                                dve.tensor_tensor(it[:, 2 * j:2 * j + 2, :],
                                                  bank[("cB", j)][:].rearrange("p (c n) -> p c n", n=N),
                                                  it[:, 2 * j:2 * j + 2, :], ALU.mult)\
                                   .then_inc(read["cB"], 1)
                            dve.wait_ge(done["y2"], b + 1)
                            wait(dve, out_stored, 16 * b)
                            dve.tensor_tensor(o_sb[:], bank[("y2", 0)][:, 0:N].rearrange("p (t d) -> p t d", d=D),
                                              x1[:], ALU.add).then_inc(read["y2"], 1)

            run_steps(dve, step)


_INS = ["L0_attn_tokens", "L0_attn_Wqg", "L0_attn_Wkv", "L0_attn_Wout", "L0_ffn_gate_kernel", "L0_ffn_gate_bias",
        "L0_ffn_w_gate", "L0_ffn_w_up", "L0_ffn_w_down", "L0_ffn_sw_gate", "L0_ffn_sw_up", "L0_ffn_sw_down"]


def kernel(**inputs):
    import numpy as np
    import concourse.bacc as bacc
    from concourse.bass_utils import run_bass_kernel_spmd

    nc = bacc.Bacc("TRN2", target_bir_lowering=False, num_devices=1)
    arrays, args = {}, []
    for name in _INS:
        a = np.ascontiguousarray(inputs[name])
        arrays[f"in_{name}"] = a
        args.append(nc.dram_tensor(f"in_{name}", a.shape, mybir.dt.from_np(a.dtype), kind="ExternalInput").ap())
    shape = inputs["L0_attn_tokens"].shape
    args.append(nc.dram_tensor("out_0", shape, F32, kind="ExternalOutput").ap())
    bass_attn_moe_layer_kernel(nc, *args)
    result = run_bass_kernel_spmd(nc, [arrays], core_ids=[0])
    return result.results[0]["out_0"]
```

```python
from contextlib import ExitStack

import concourse.bass as bass
from concourse import mybir

F32 = mybir.dt.float32
F32R = mybir.dt.float32r
I32 = mybir.dt.int32
ALU = mybir.AluOpType
ACT = mybir.ActivationFunctionType
AX = mybir.AxisListType

P = 128
EPS_LN = 1e-5
TINY = 1e-35
INV_EPS = 1e12
RSQRT_MAGIC = 1597463007.0
SCALE = 2.5
REPLACED = -3.0e38
SENTINEL = -2.0e38


def bass_attn_moe_layer_kernel(nc, tokens, Wqg, Wkv, Wout, gate_kernel, gate_bias,
                               w_gate, w_up, w_down, sw_gate, sw_up, sw_down, out):
    B, N, D = tokens.shape
    E, _, M = w_gate.shape
    T = N // P
    DV = 64
    H = Wout.shape[0] // DV
    DK = Wqg.shape[1] // H - DV
    NP = H // 2
    EC = E // 2
    FC = EC + 1
    NG = 4
    EG = E // NG
    TOP_K = 4
    HK = H * DK
    HV = H * DV
    SLOTS = NP
    assert D == P and T == 2 and DK == 16 and 2 * M == P and 2 * DV == P and H == E == 16 and FC == 9

    SKIP = ("-", "skip", 0)
    FILL = [
        [("P", "qk", 0), ("P", "qk", 1), ("P", "v", 0), ("P", "v", 1), ("O", "ones", 0), ("F", "lg", 0)],
        [("P", "v", 2), ("P", "v", 3), ("O", "nT", 0), ("F", "gu", 0), ("F", "gu", 1), ("F", "gu", 2)],
        [("F", "gu", 3), ("F", "gu", 4), ("F", "gu", 5), ("F", "gu", 6), ("P", "g", 0)],
        [("F", "gu", 7), ("P", "g", 1), ("F", "gu", 8), ("P", "g", 2), ("O", "rT", 0)],
        [("O", "rB", j) for j in range(4)] + [("P", "tr", 0), ("P", "tr", 1), ("P", "tr", 2), ("P", "g", 3)],
        [("O", "y", 0), ("O", "y", 1), ("P", "tr", 3), SKIP, SKIP],
        [("F", "cT", 0), ("P", "tr", 4), ("P", "tr", 5)] + [("F", "cB", j) for j in range(4)]
        + [("P", "tr", 6), ("P", "tr", 7)],
        [("F", "y2", 0), ("O", "x2T", 0), ("L", "xT", 0), ("F", "y2", 1)],
    ]
    ORDER = [job for slot in FILL for job in slot]
    assert len(FILL) == SLOTS and len(ORDER) % 4 == 0
    OFFSET = {"L": 2, "P": 1, "A": 0, "O": -1, "F": -2}
    JOBS = {"xT": 1, "qk": 2, "v": 4, "g": 4, "tr": NP, "ones": 1, "nT": 1, "rT": 1, "rB": 4, "y": 2,
            "x2T": 1, "lg": 1, "gu": FC, "cT": 1, "cB": 4, "y2": 2}

    def stages(s):
        return {k for k, d in OFFSET.items() if 0 <= s + d < B}

    ALL = set(OFFSET)
    FIRST_STEP, LOOP_FROM, LOOP_TO, LAST_STEP = -2, 4, B - 2, B + 1
    assert all(stages(s) == ALL for s in range(LOOP_FROM - 1, LOOP_TO)) and (LOOP_TO - LOOP_FROM) % 2 == 0

    with ExitStack() as ctx:
        def sb(name, shape, dt=F32):
            return ctx.enter_context(nc.sbuf_tensor(name, shape, dt))

        def sem(name):
            return ctx.enter_context(nc.semaphore(name))

        wqk = [sb(f"wqk_{k}", [P, 2 * HK], F32R) for k in ("hi", "lo")]
        wv = [sb(f"wv_{k}", [P, HV], F32R) for k in ("hi", "lo")]
        wg = [sb(f"wg_{k}", [P, HV], F32R) for k in ("hi", "lo")]
        weg = [sb(f"weg_{k}", [P, FC * P], F32R) for k in ("hi", "lo")]
        weu = [sb(f"weu_{k}", [P, FC * P], F32R) for k in ("hi", "lo")]
        wout = sb("wout", [P, NP, D])
        wdown = sb("wdown", [P, FC, D])
        wroute = sb("wroute", [P, E])
        bias = sb("bias", [P, E])
        ident = sb("ident", [P, P])
        ones32 = sb("ones32", [P, 2, 32])
        pick = sb("pick", [P, H])
        sel = sb("sel", [2 * H, NP, P], F32R)
        lower = sb("lower", [P, NG, NG])
        RAW = 2 * (HK + HV) + 2 * FC * P
        big = sb("big", [P, max(RAW, 3 * NP * N)])
        aw = [big[:, q * NP * N:(q + 1) * NP * N].rearrange("p (c n) -> p c n", n=N) for q in range(2)]
        a2 = big[:, 2 * NP * N:3 * NP * N].rearrange("p (c n) -> p c n", n=N)
        x_in = [sb(f"x_in{q}", [P, T, D]) for q in range(2)]
        x_res = [sb(f"x_res{q}", [P, T, D]) for q in range(2)]
        xn = sb("xn", [P, T, D])
        xh, xl = sb("xh", [P, N], F32R), sb("xl", [P, N], F32R)
        qk = sb("qk", [P, T, 2 * HK])
        qks = sb("qks", [P, T, 2 * H, 4, DK], F32R)
        qkt = [sb(f"qkt{q}", [P, NP, 2 * N], F32R) for q in range(2)]
        v = [sb(f"v{q}", [P, T, HV]) for q in range(2)]
        wt = [sb(f"wt{q}", [P, NP, N]) for q in range(2)]
        r = [sb(f"r{k}", [P, 2 * N]) for k in range(2)]
        p = [sb(f"p{k}", [P, 2 * N]) for k in range(4)]
        rs = sb("rs", [P, T, 2, H])
        rt = sb("rt", [2 * H, N], F32R)
        sq = sb("sq", [P, HV])
        selraw = sq[0:2 * H, :].rearrange("p (c n) -> p c n", n=P)
        x1 = [sb(f"x1_{q}", [P, T, D]) for q in range(2)]
        n2row = [x1[q][:].rearrange("p t d -> p (t d)") for q in range(2)]
        xn2 = sb("xn2", [P, T, D])
        x2h, x2l = sb("x2h", [P, N], F32R), sb("x2l", [P, N], F32R)
        sg = [sb(f"sg{k}", [P, N]) for k in range(2)]
        it = sb("it", [P, FC, N])
        cs = sb("cs", [P, T, 2, E])
        o_sb = sb("o_sb", [P, T, D])

        def norm_tiles(name, n):
            return {k: sb(f"{name}_{k}", [P, n]) for k in ("m", "y", "t")}

        st1, mv1 = sb("st1", [P, T, 6]), sb("mv1", [P, T, 2])
        st2, mv2 = sb("st2", [P, T, 6]), sb("mv2", [P, T, 2])
        ln = norm_tiles("ln", 2 * T)
        S3 = 2 * H + H
        NS = T * S3
        ss, nt = sb("ss", [P, NS + T * H]), norm_tiles("norms", NS + T * H)
        ss3 = ss[:, 0:NS].rearrange("p (t h) -> p t h", t=T)
        rn3 = nt["y"][:, 0:NS].rearrange("p (t h) -> p t h", t=T)
        n2, rn2 = ss[:, NS:], nt["y"][:, NS:]
        rk2, vs = sb("rk2", [P, T, H]), sb("vs", [P, T, H])
        rq2 = [sb(f"rq2_{q}", [P, T, H]) for q in range(2)]
        nn, tn, bound = sb("nn", [P, T * H]), sb("tn", [P, T * H]), sb("bound", [P, T * H])
        rr = sb("rr", [P, T * H])
        th, sc = sb("th", [P, T * E]), sb("sc", [P, T * E])
        pairs, gsum = sb("pairs", [P, T * NG, 6]), sb("gsum", [P, T * NG])
        gt, eq = sb("gt", [P, T, NG, NG]), sb("eq", [P, T, NG, NG])
        rank = sb("rank", [P, T * NG])
        masked = sb("masked", [P, T * NG, EG])
        EB = E + 8
        cand, repl = sb("cand", [P, T, EB]), sb("repl", [P, T, EB])
        top = sb("top", [P, T, 8])
        chosen = sb("chosen", [P, T, E])
        den, comb = sb("den", [P, T]), sb("comb", [P, T, E])
        split_hi = sb("split_hi", [P, T, H], F32R)
        carrier = sb("carrier", [P, 1])

        ps_s = [ctx.enter_context(nc.psum_tensor(f"ps_s{k}", [P, 512], F32)) for k in range(2)]
        ps_a = [ctx.enter_context(nc.psum_tensor(f"ps_a{k}", [P, 512], F32)) for k in range(2)]
        ps_f = [ctx.enter_context(nc.psum_tensor(f"ps_f{k}", [P, 512], F32)) for k in range(4)]
        bank = {job[1:]: ps_f[n % 4] for n, job in enumerate(ORDER) if job != SKIP}

        x_loaded = [sem(f"x_loaded{q}") for q in range(2)]
        w_loaded = [sem(f"w_loaded{k}") for k in range(3)]
        c_loaded = sem("c_loaded")
        out_stored = sem("out_stored")
        consts_pool, consts_dve = sem("consts_pool"), sem("consts_dve")
        w_hi, w_lo = sem("w_hi"), sem("w_lo")
        done = {k: sem(f"{k}_done") for k in JOBS}
        read = {k: sem(f"{k}_read") for k in JOBS}
        scores_done, values_done = sem("scores_done"), sem("values_done")
        relu_done, probs_done = sem("relu_done"), sem("probs_done")
        a2_done, aw_done = sem("a2_done"), sem("aw_done")
        ln1_ready, xh_ready, x_kept = sem("ln1_ready"), sem("xh_ready"), sem("x_kept")
        sums_done, vs_ready, v_normed = sem("sums_done"), sem("vs_ready"), sem("v_normed")
        qk_hi, qk_lo = sem("qk_hi"), sem("qk_lo")
        gate_ready = sem("gate_ready")
        n_ready, tanh_n, r_ready = sem("n_ready"), sem("tanh_n"), sem("r_ready")
        ln2_ready, x2h_ready = sem("ln2_ready"), sem("x2h_ready")
        silu_done, c_ready = sem("silu_done"), sem("c_ready")
        ch_l, ch_p, ch_o, ch_n, ch_f = (sem(f"ch_{k}") for k in "lponf")
        ch_norms, ch_ln = sem("ch_norms"), sem("ch_ln")

        block = ctx.enter_context(nc.Block())

        def run_steps(eng, step):
            for s in range(FIRST_STEP, LOOP_FROM):
                step(s, s % 2, stages(s), s)
            with eng.Fori(LOOP_FROM // 2, LOOP_TO // 2) as i:
                step(i * 2, 0, ALL, None)
                step(i * 2 + 1, 1, ALL, None)
            for s in range(LOOP_TO, LAST_STEP + 1):
                step(s, s % 2, stages(s), s)

        def wait(eng, semaphore, value):
            if not isinstance(value, int) or value > 0:
                eng.wait_ge(semaphore, value)

        def at_most(value, most):
            return min(value, most) if isinstance(value, int) else value

        def broadcast(ap, shape, at):
            return ap.unsqueeze(at).broadcast_to(shape)

        def slots_of(part, t):
            heads = qks[:, t, H * part:H * part + H, :, :]
            if part == 0:
                heads = heads.rearrange("p h (r a) d -> p a h r d", a=2)
            else:
                heads = heads.rearrange("p h (a r) d -> p a h r d", a=2)
            whole = qk[:, t, HK * part:HK * part + HK].rearrange("p (h d) -> p h d", d=DK)
            return heads[:, 0], heads[:, 1], broadcast(whole, [P, H, 2, DK], 2)

        @block.sync
        def _(sp):
            def load_x(b, q):
                sp.dma_start(x_in[q][:], tokens[b].rearrange("(t p) d -> p t d", p=P)).then_inc(x_loaded[q], 16)

            load_x(0, 0)
            sp.dma_start(big[:, 0:HK + HV], Wqg).then_inc(w_loaded[0], 16)
            sp.dma_start(big[:, HK + HV:2 * (HK + HV)], Wkv).then_inc(w_loaded[0], 16)
            load_x(1, 1)
            base = 2 * (HK + HV)
            for w, sw in ((w_gate, sw_gate), (w_up, sw_up)):
                k = 1 if w is w_gate else 2
                sp.dma_start(big[:, base:base + E * M].rearrange("p (e m) -> p e m", m=M),
                             w.rearrange("e h m -> h e m")).then_inc(w_loaded[k], 16)
                sp.dma_start(big[:, base + E * M:base + FC * P], sw).then_inc(w_loaded[k], 16)
                base += FC * P
            sp.dma_start(wout[:], Wout.rearrange("(c p) n -> p c n", p=P)).then_inc(c_loaded, 16)
            sp.dma_start(wdown[:, 0:EC, :], w_down.rearrange("(c e) m h -> (e m) c h", e=2)).then_inc(c_loaded, 16)
            sp.dma_start(wdown[:, EC, :], sw_down).then_inc(c_loaded, 16)
            sp.dma_start(wroute[:], gate_kernel).then_inc(c_loaded, 16)
            sp.dma_start(bias[:], gate_bias.rearrange("(a e) -> a e", a=1).broadcast_to([P, E])).then_inc(c_loaded, 16)

            def step(s, q, on, at):
                if "L" in on and "A" in on:
                    sp.wait_ge(x_kept, s + 1)
                    sp.wait_ge(ln1_ready, s + 1)
                    load_x(s + 2, q)
                if "F" in on:
                    sp.wait_ge(read["y2"], (s - 1) * 2)
                    sp.dma_start(out[s - 2].rearrange("(t p) d -> p t d", p=P), o_sb[:])\
                      .then_inc(out_stored, 16)

            run_steps(sp, step)
            sp.wait_ge(out_stored, 16 * B)

        @block.gpsimd
        def _(pool):
            n = [0]

            def built(ins):
                n[0] += 1
                ins.then_inc(consts_pool, 1)
                pool.wait_ge(consts_pool, n[0])

            built(pool.memset(ident[:], 0.0))
            built(pool.affine_select(out=ident[:], in_=ident[:], compare_op=ALU.not_equal, fill=1.0, base=0,
                                     pattern=[[-1, P]], channel_multiplier=1))
            built(pool.memset(selraw, 0.0))
            for part in range(2):
                view = selraw.rearrange("k c (e m) -> k c e m", e=2)
                built(pool.affine_select(out=view, in_=view, compare_op=ALU.not_equal, fill=1.0, base=-H * part,
                                         pattern=[[-2, NP], [-1, 2], [0, DV]], channel_multiplier=1))
            built(pool.memset(pick[:], 0.0))
            view = pick[:].rearrange("p (a j e) -> p a j e", j=4, e=2)
            built(pool.affine_select(out=view, in_=view, compare_op=ALU.not_equal, fill=1.0, base=0,
                                     pattern=[[-2, 2], [-32, 4], [-1, 2]], channel_multiplier=1))

            def step(s, q, on, at):
                for k in range(SLOTS):
                    if "A" in on:
                        for h in (2 * k, 2 * k + 1):
                            wait(pool, values_done, 8 * s + (h - 4) // 2 + 1)
                            pool.wait_ge(relu_done, 16 * s + h + 1)
                            pool.tensor_tensor(p[h % 4][:], r[h % 2][:], r[h % 2][:], ALU.mult).then_inc(probs_done, 1)
                    if "P" in on:
                        b = s + 1
                        if k in (2, 3):
                            t = k - 2
                            wait(pool, done["tr"], 8 * b)
                            for part in range(2):
                                pool.wait_ge(qk_hi, 4 * b + 2 * t + part + 1)
                                hi, lo, whole = slots_of(part, t)
                                pool.tensor_tensor(lo, whole, hi.bitcast(F32), ALU.subtract).then_inc(qk_lo, 1)
                        if k in (4, 5, 6, 7):
                            t, half = divmod(k - 4, 2)
                            pool.wait_ge(vs_ready, b + 1)
                            pool.wait_ge(read["v"], 4 * b + k - 3)
                            view = v[1 - q][:, t, half * 512:(half + 1) * 512].rearrange("p (h d) -> p h d", d=DV)
                            scale = vs[:, t, half * NP:(half + 1) * NP]
                            pool.tensor_tensor(view, view, broadcast(scale, [P, NP, DV], 2), ALU.mult)\
                                .then_inc(v_normed, 1)

            run_steps(pool, step)

        @block.tensor
        def _(pe):
            pe.wait_ge(consts_pool, 7)
            pe.wait_ge(consts_dve, 2)
            weights = {"qk": 2, "v": 3, "g": 4, "gu": 6, "lg": 7, "y": 7, "y2": 7}

            def three(dst, stat, mov):
                pe.matmul(dst, stat[0], mov[0], start=True, stop=False)
                pe.matmul(dst, stat[0], mov[1], start=False, stop=False)
                return pe.matmul(dst, stat[1], mov[0], start=False, stop=True)

            def filler(stage, kind, j, s, q, at):
                b = s + OFFSET[stage]
                ps = bank[(kind, j)]
                pb = 1 - q
                if at is not None and kind in weights:
                    pe.wait_ge(w_lo, weights[kind])
                tok = [slice(t * P, (t + 1) * P) for t in range(T)]
                if kind == "xT":
                    pe.wait_ge(ln1_ready, b + 1)
                    for t in range(T):
                        last = pe.transpose(ps[:, tok[t]], xn[:, t, :], ident[:])
                elif kind == "qk":
                    if j == 0:
                        pe.wait_ge(xh_ready, b + 1)
                        pe.wait_ge(read["xT"], b + 1)
                    last = three(ps[:, 0:2 * HK], (xh[:, tok[j]], xl[:, tok[j]]), (wqk[0][:], wqk[1][:]))
                elif kind == "v":
                    half = slice((j % 2) * 512, (j % 2 + 1) * 512)
                    last = three(ps[:, :], (xh[:, tok[j // 2]], xl[:, tok[j // 2]]), (wv[0][:, half], wv[1][:, half]))
                elif kind == "g":
                    for c in range(2):
                        cols = slice((2 * j + c) * P, (2 * j + c + 1) * P)
                        last = three(ps[:, c * N:(c + 1) * N], (wg[0][:, cols], wg[1][:, cols]), (xh[:], xl[:]))
                elif kind == "tr":
                    if j == 0:
                        pe.wait_ge(qk_lo, 4 * b + 4)
                    for part in range(2):
                        for t in range(T):
                            src = qks[:, t, H * part + 2 * j:H * part + 2 * j + 2, :, :].bitcast(F32)
                            src = src.rearrange("p h a d -> p (h a d)")
                            last = pe.transpose(ps[:, part * N + t * P:part * N + (t + 1) * P], src, ident[:])
                elif kind == "ones":
                    pe.wait_ge(a2_done, 8 * b + 8)
                    for a in range(2):
                        for c in range(4):
                            last = pe.matmul(ps[32 * c:32 * c + 32, 0:N], ones32[:, a, :], a2[:, 4 * a + c, :],
                                             start=(a == 0), stop=(a == 1))
                elif kind == "nT":
                    pe.wait_ge(read["ones"], b + 1)
                    for t in range(T):
                        last = pe.matmul(ps[:, t * H:(t + 1) * H], n2row[pb][:, tok[t]], pick[:], start=True, stop=True)
                elif kind in ("rT", "cT"):
                    pe.wait_ge(r_ready if kind == "rT" else c_ready, b + 1)
                    src = rs if kind == "rT" else cs
                    for t in range(T):
                        last = pe.transpose(ps[0:2 * H, tok[t]], src[:, t, :, :].rearrange("p a h -> p (a h)"), ident[:])
                elif kind in ("rB", "cB"):
                    ready = read["rT" if kind == "rB" else "cT"]
                    if j == 0:
                        pe.wait_ge(ready, b + 1)
                    for c in range(2):
                        last = pe.matmul(ps[:, c * N:(c + 1) * N], sel[:, 2 * j + c, :], rt[:], start=True, stop=True)
                elif kind == "y":
                    pe.wait_ge(read["rB"], 4 * b + 4)
                    for c in range(NP):
                        last = pe.matmul(ps[:, 0:D], aw[pb][:, c, tok[j]], wout[:, c, :],
                                         start=(c == 0), stop=(c == NP - 1))
                elif kind == "x2T":
                    pe.wait_ge(ln2_ready, b + 1)
                    for t in range(T):
                        last = pe.transpose(ps[:, tok[t]], xn2[:, t, :], ident[:])
                elif kind == "lg":
                    pe.wait_ge(x2h_ready, b + 1)
                    pe.wait_ge(read["x2T"], b + 1)
                    for t in range(T):
                        pe.matmul(ps[:, t * E:(t + 1) * E], x2h[:, tok[t]].bitcast(F32), wroute[:], start=True, stop=False)
                        last = pe.matmul(ps[:, t * E:(t + 1) * E], x2l[:, tok[t]].bitcast(F32), wroute[:],
                                         start=False, stop=True)
                elif kind == "gu":
                    cols = slice(j * P, (j + 1) * P)
                    three(ps[:, 0:N], (weg[0][:, cols], weg[1][:, cols]), (x2h[:], x2l[:]))
                    last = three(ps[:, N:2 * N], (weu[0][:, cols], weu[1][:, cols]), (x2h[:], x2l[:]))
                else:
                    pe.wait_ge(read["cB"], 4 * b + 4)
                    for c in range(FC):
                        last = pe.matmul(ps[:, 0:D], it[:, c, tok[j]], wdown[:, c, :],
                                         start=(c == 0), stop=(c == FC - 1))
                last.then_inc(done[kind], 1)

            def wait_for_bank(n, s, at):
                m, d = n - 4, 0
                while True:
                    if m < 0:
                        m, d = m + len(ORDER), d - 1
                    stage, kind, j = ORDER[m]
                    if stage in (ALL if at is None else stages(at + d)):
                        break
                    if at is not None and at + d < FIRST_STEP:
                        return
                    m -= 4
                wait(pe, read[kind], (s + d + OFFSET[stage]) * JOBS[kind] + j + 1)

            def step(s, q, on, at):
                n = 0
                for k in range(SLOTS):
                    if "A" in on:
                        if k == 0:
                            pe.wait_ge(read["tr"], 8 * s + 8)
                        for t in range(T):
                            for e in range(2):
                                if t == 0:
                                    wait(pe, relu_done, 16 * s + 2 * k + e - 1)
                                rows = slice(64 * e, 64 * e + 64)
                                last = pe.matmul(ps_s[e][:, t * N:(t + 1) * N],
                                                 qkt[q][rows, k, N + t * P:N + (t + 1) * P], qkt[q][rows, k, 0:N],
                                                 start=True, stop=True)
                                if t == T - 1:
                                    last.then_inc(scores_done, 1)
                    for stage, kind, j in FILL[k]:
                        if stage in on:
                            wait_for_bank(n, s, at)
                            filler(stage, kind, j, s, q, at)
                        n += 1
                    if "A" in on:
                        wait(pe, aw_done, 8 * s + k - 1)
                        if k == 0:
                            pe.wait_ge(v_normed, 4 * s + 4)
                        for t in range(T):
                            for e in range(2):
                                h = 2 * k + e
                                if t == 0:
                                    pe.wait_ge(probs_done, 16 * s + h + 1)
                                last = pe.matmul(ps_a[k % 2][64 * e:64 * e + 64, 0:N],
                                                 v[q][:, t, h * DV:(h + 1) * DV], p[h % 4][:, t * N:(t + 1) * N],
                                                 start=(t == 0), stop=(t == T - 1))
                        last.then_inc(values_done, 1)

            run_steps(pe, step)

        @block.scalar
        def _(act):
            act.wait_ge(w_loaded[0], 32)
            gq = big[:, 0:HK + HV].rearrange("p (h c) -> p h c", h=H)
            kv = big[:, HK + HV:2 * (HK + HV)].rearrange("p (h c) -> p h c", h=H)
            base = 2 * (HK + HV)

            def heads(w, c):
                return w.rearrange("p (h c) -> p h c", c=c)

            act.activation(heads(wqk[0][:, 0:HK], DK), gq[:, :, 0:DK], ACT.Copy).then_inc(w_hi, 1)
            act.activation(heads(wqk[0][:, HK:2 * HK], DK), kv[:, :, 0:DK], ACT.Copy).then_inc(w_hi, 1)
            act.activation(heads(wv[0][:], DV), kv[:, :, DK:], ACT.Copy).then_inc(w_hi, 1)
            act.activation(heads(wg[0][:], DV), gq[:, :, DK:], ACT.Copy).then_inc(w_hi, 1)
            act.wait_ge(consts_dve, 2)

            def expert_weights():
                act.wait_ge(w_loaded[1], 32)
                act.activation(weg[0][:], big[:, base:base + FC * P], ACT.Copy).then_inc(w_hi, 1)
                act.wait_ge(w_loaded[2], 32)
                act.activation(weu[0][:], big[:, base + FC * P:base + 2 * FC * P], ACT.Copy).then_inc(w_hi, 1)

            def squares(j, b, ps, kind):
                wait(act, sums_done, 6 * b + j - 1)
                act.activation(sq[:, (j % 2) * 512:(j % 2 + 1) * 512], ps[:], ACT.Square).then_inc(read[kind], 1)

            def gates(j, s, q):
                b = s + 1
                dst = wt[1 - q][:, 2 * j:2 * j + 2, :]
                act.wait_ge(read["g"], 4 * b + j + 1)
                act.activation(dst, dst, ACT.Tanh).then_inc(gate_ready, 1)

            def evacuate(stage, kind, j, s, q):
                b = s + OFFSET[stage]
                pq = 1 - q
                ps = bank[(kind, j)]
                count = b * JOBS[kind] + j + 1
                if kind == "xT":
                    wait(act, done["g"], 4 * b)
                    act.wait_ge(done[kind], count)
                    act.activation(xh[:], ps[:, 0:N], ACT.Copy).then_inc(xh_ready, 1)
                elif kind == "qk":
                    wait(act, qk_lo, 4 * b)
                    act.wait_ge(done[kind], count)
                    act.activation(qk[:, j, :], ps[:, 0:2 * HK], ACT.Copy)
                    squares(j, b, ps, kind)
                elif kind == "v":
                    if j == 0:
                        wait(act, values_done, 8 * (b - 1))
                    act.wait_ge(done[kind], count)
                    act.activation(v[pq][:, j // 2, (j % 2) * 512:(j % 2 + 1) * 512], ps[:], ACT.Copy)
                    squares(j + 2, b, ps, kind)
                elif kind == "g":
                    if j == 0:
                        wait(act, aw_done, 8 * (b - 1))
                    act.wait_ge(done[kind], count)
                    dst = wt[pq][:, 2 * j:2 * j + 2, :]
                    act.activation(dst, ps[:].rearrange("p (c n) -> p c n", n=N), ACT.Silu).then_inc(read[kind], 1)
                elif kind == "tr":
                    if j == 0:
                        wait(act, scores_done, 16 * (b - 1))
                    act.wait_ge(done[kind], count)
                    act.activation(qkt[pq][:, j, :], ps[:], ACT.Copy).then_inc(read[kind], 1)
                elif kind == "ones":
                    wait(act, read["y2"], 2 * (b - 1))
                    act.wait_ge(done[kind], count)
                    act.activation(n2row[pq], ps[:, 0:N], ACT.Copy).then_inc(read[kind], 1)
                elif kind in ("rT", "cT"):
                    if kind == "rT":
                        wait(act, done["cB"], 4 * (b - 1))
                    else:
                        act.wait_ge(done["rB"], at_most(4 * (b + 2), 4 * B))
                    act.wait_ge(done[kind], count)
                    act.activation(rt[:], ps[0:2 * H, 0:N], ACT.Copy).then_inc(read[kind], 1)
                elif kind == "x2T":
                    wait(act, done["gu"], FC * b)
                    act.wait_ge(done[kind], count)
                    act.activation(x2h[:], ps[:, 0:N], ACT.Copy).then_inc(x2h_ready, 1)
                elif kind == "lg":
                    act.wait_ge(done[kind], count)
                    act.activation(th[:], ps[:, 0:T * E], ACT.Tanh, scale=0.5).then_inc(read[kind], 1)
                elif kind == "gu":
                    wait(act, read["gu"], FC * b + j - 1)
                    act.wait_ge(done[kind], count)
                    act.activation(sg[j % 2][:], ps[:, 0:N], ACT.Silu).then_inc(silu_done, 1)

            def step(s, q, on, at):
                for k in range(SLOTS):
                    if "A" in on:
                        for h in (2 * k, 2 * k + 1):
                            wait(act, probs_done, 16 * s + h - 1)
                            act.wait_ge(scores_done, 16 * s + h + 1)
                            act.activation(r[h % 2][:], ps_s[h % 2][:], ACT.Relu).then_inc(relu_done, 1)
                    if ("A" in on and k > 0) or ("O" in on and k == 0):
                        pair, b = (k - 1, s) if k > 0 else (NP - 1, s - 1)
                        if pair == 0:
                            wait(act, done["ones"], s)
                            if at == 0:
                                act.wait_ge(w_lo, 6)
                        act.wait_ge(values_done, 8 * b + pair + 1)
                        act.activation(a2[:, pair, :], ps_a[pair % 2][:, 0:N], ACT.Square).then_inc(a2_done, 1)
                    if k == 3 and "O" in on:
                        act.wait_ge(n_ready, s)
                        act.activation(tn[:], nn[:], ACT.Tanh).then_inc(tanh_n, 1)
                    for stage, kind, j in FILL[k - 1] if k > 0 else ():
                        if kind == "g" and stage in on:
                            gates(j, s, q)
                    for stage, kind, j in FILL[k]:
                        if stage in on:
                            evacuate(stage, kind, j, s, q)
                    if k in (1, 2) and "P" in on:
                        b, t = s + 1, k - 1
                        wait(act, done["tr"], 8 * b)
                        act.wait_ge(read["qk"], 2 * b + t + 1)
                        for part in range(2):
                            hi, _, whole = slots_of(part, t)
                            act.activation(hi, whole, ACT.Copy).then_inc(qk_hi, 1)
                if at == -1:
                    expert_weights()

            run_steps(act, step)

        @block.vector
        def _(dve):
            class Chain:

                def __init__(self, semaphore, per, b):
                    self.semaphore, self.per, self.b, self.n = semaphore, per, b, 0

                def __call__(self, ins, apart=False):
                    self.n += 1
                    assert self.n <= self.per
                    ins.then_inc(self.semaphore, 1)
                    dve.wait_ge(self.semaphore, self.b * self.per + self.n)
                    if apart:
                        dve.memset(carrier[:], 0.0)

                def end(self):
                    assert self.n == self.per, self.n

            def seed(link, tiles):
                m, y = tiles["m"][:], tiles["y"][:]
                link(dve.tensor_single_scalar(y.bitcast(I32), m.bitcast(I32), 1, ALU.logical_shift_right))
                link(dve.tensor_scalar(y.bitcast(I32), y.bitcast(I32), -1.0, RSQRT_MAGIC, ALU.mult, ALU.add))

            def newton(link, tiles):
                m, y, t = tiles["m"][:], tiles["y"][:], tiles["t"][:]
                link(dve.tensor_tensor(t, y, y, ALU.mult))
                link(dve.scalar_tensor_tensor(out=t, in0=t, scalar=-0.5, in1=m, op0=ALU.mult, op1=ALU.mult))
                link(dve.scalar_tensor_tensor(out=y, in0=t, scalar=1.5, in1=y, op0=ALU.add, op1=ALU.mult))

            RS_OPS = 11
            LN_OPS, NORM_OPS, P_OPS, O_OPS, F_OPS = RS_OPS, RS_OPS + 1, 2, 4, 21

            def row_stats(link, x, st, mv, part):
                for t in range(T):
                    last = dve.bn_stats(st[:, t, :], x[:, t, :])
                link(last, apart=True)
                for t in range(T):
                    last = dve.bn_aggr(mv[:, t, :], st[:, t, :])
                link(last)
                link(dve.tensor_scalar(ln["m"][:, part * T:part * T + T], mv[:, :, 1], EPS_LN, None, ALU.add))

            def normed_rows(x, mv, part, dst, ready):
                for t in range(T):
                    last = dve.tensor_scalar(dst[:, t, :], x[:, t, :], mv[:, t, 0:1],
                                             ln["y"][:, part * T + t:part * T + t + 1], ALU.subtract, ALU.mult)
                last.then_inc(ready, 1)

            n = [0]

            def built(ins):
                n[0] += 1
                ins.then_inc(consts_dve, 1)
                dve.wait_ge(consts_dve, n[0])

            dve.wait_ge(consts_pool, 7)
            dve.tensor_copy(sel[:], selraw)
            dve.memset(ones32[:], 0.0)
            dve.memset(ss[:], 1.0)
            dve.memset(ln["m"][:], 1.0)
            dve.memset(lower[:], 0.0)
            built(dve.memset(cand[:], SENTINEL))
            for e in range(2):
                for a in range(2):
                    dve.memset(ones32[64 * e:64 * e + 64, a, 2 * a + e:2 * a + e + 1], 1.0)
            for g in range(1, NG):
                last = dve.memset(lower[:, g, 0:g], 1.0)
            built(last)

            gq = big[:, 0:HK + HV].rearrange("p (h c) -> p h c", h=H)
            kv = big[:, HK + HV:2 * (HK + HV)].rearrange("p (h c) -> p h c", h=H)
            base = 2 * (HK + HV)

            def rest(k, w, raw, c):
                dve.wait_ge(w_hi, k)
                lo, hi = w[1], w[0]
                if c:
                    lo, hi = lo.rearrange("p (h c) -> p h c", c=c), hi.rearrange("p (h c) -> p h c", c=c)
                dve.tensor_tensor(lo, raw, hi.bitcast(F32), ALU.subtract).then_inc(w_lo, 1)

            def projection_weights():
                rest(1, [w[:, 0:HK] for w in wqk], gq[:, :, 0:DK], DK)
                rest(2, [w[:, HK:2 * HK] for w in wqk], kv[:, :, 0:DK], DK)
                rest(3, [w[:] for w in wv], kv[:, :, DK:], DV)
                rest(4, [w[:] for w in wg], gq[:, :, DK:], DV)

            def expert_weights():
                rest(5, [w[:] for w in weg], big[:, base:base + FC * P], 0)
                rest(6, [w[:] for w in weu], big[:, base + FC * P:base + 2 * FC * P], 0)
                dve.wait_ge(c_loaded, 80)
                dve.tensor_copy(th[:, 0:E], bias[:]).then_inc(w_lo, 1)

            def sums(j, b):
                if j < 2:
                    dve.wait_ge(read["qk"], 2 * b + j + 1)
                    dst, d = ss3[:, j, 0:2 * H], DK
                else:
                    t, half = divmod(j - 2, 2)
                    dve.wait_ge(read["v"], 4 * b + j - 1)
                    dst, d = ss3[:, t, 2 * H + half * NP:2 * H + (half + 1) * NP], DV
                dve.tensor_reduce(dst, sq[:, (j % 2) * 512:(j % 2 + 1) * 512].rearrange("p (h d) -> p h d", d=d),
                                  AX.X, ALU.add).then_inc(sums_done, 1)

            def norms_start(link, P_on, O_on, s):
                if P_on:
                    dve.wait_ge(sums_done, 6 * s + 12)
                if O_on:
                    dve.wait_ge(read["nT"], s)
                link(dve.tensor_scalar(nt["m"][:], ss[:], TINY, None, ALU.max))
                seed(link, nt)

            def head_norms(link, b, c):
                c = c[:].rearrange("p t h -> p (t h)")
                link(dve.tensor_tensor(nn[:], n2, rn2, ALU.mult))
                dve.tensor_tensor(nn[:], nn[:], c, ALU.mult).then_inc(n_ready, 1)
                link(dve.scalar_tensor_tensor(out=bound[:], in0=c, scalar=INV_EPS, in1=rn2, op0=ALU.mult, op1=ALU.min))
                dve.wait_ge(n_ready, b + 1)

            def value_scales(link, b, c):
                link(dve.tensor_scalar(rn3, rn3, INV_EPS, None, ALU.min))
                dve.tensor_tensor(c[:], rn3[:, :, 0:H], rn3[:, :, 0:H], ALU.mult)
                link(dve.tensor_tensor(rk2[:], rn3[:, :, H:2 * H], rn3[:, :, H:2 * H], ALU.mult))
                wait(dve, v_normed, 4 * b)
                dve.tensor_tensor(vs[:], rn3[:, :, 2 * H:S3], rk2[:], ALU.mult).then_inc(vs_ready, 1)

            def head_scales(link, b):
                dve.wait_ge(tanh_n, b + 1)
                link(dve.tensor_tensor(rr[:], tn[:], bound[:], ALU.mult))
                split(link, rs, rr[:].rearrange("p (t h) -> p t h", t=T), r_ready)

            def split(link, dst, src, ready):
                link(dve.tensor_copy(split_hi[:], src))
                dve.tensor_copy(dst[:, :, 0, :], split_hi[:].bitcast(F32))
                dve.tensor_tensor(dst[:, :, 1, :], src, split_hi[:].bitcast(F32), ALU.subtract).then_inc(ready, 1)

            def route_groups(link, b):
                dve.wait_ge(read["lg"], b + 1)
                link(dve.tensor_scalar(sc[:], th[:], 0.5, 0.5, ALU.mult, ALU.add))
                link(dve.tensor_tensor(sc[:].rearrange("p (t e) -> p t e", t=T), sc[:].rearrange("p (t e) -> p t e", t=T),
                                       broadcast(bias[:], [P, T, E], 1), ALU.add))
                s4 = sc[:].rearrange("p (g e) -> p g e", e=EG)
                dve.tensor_tensor(pairs[:, :, 0:3], s4[:, :, 0:3], s4[:, :, 1:4], ALU.add)
                dve.tensor_tensor(pairs[:, :, 3:5], s4[:, :, 0:2], s4[:, :, 2:4], ALU.add)
                link(dve.tensor_tensor(pairs[:, :, 5:6], s4[:, :, 0:1], s4[:, :, 3:4], ALU.add))
                link(dve.tensor_reduce(gsum[:], pairs[:], AX.X, ALU.max))
                gs = gsum[:].rearrange("p (t g) -> p t g", t=T)
                other, own = broadcast(gs, [P, T, NG, NG], 2), broadcast(gs, [P, T, NG, NG], 3)
                dve.tensor_tensor(gt[:], other, own, ALU.is_gt)
                link(dve.tensor_tensor(eq[:], other, own, ALU.is_equal))
                link(dve.tensor_tensor(eq[:], eq[:], broadcast(lower[:], [P, T, NG, NG], 1), ALU.mult))
                link(dve.tensor_tensor(gt[:], gt[:], eq[:], ALU.add))
                link(dve.tensor_reduce(rank[:].rearrange("p (t g) -> p t g", t=T), gt[:], AX.X, ALU.add))
                link(dve.tensor_scalar(rank[:], rank[:], 2.0, None, ALU.is_lt))
                link(dve.tensor_tensor(masked[:], s4, broadcast(rank[:], [P, T * NG, EG], 2), ALU.mult))
                link(dve.tensor_scalar(cand[:, :, 0:E], masked[:].rearrange("p (t g) e -> p t (g e)", t=T), 0.0, None,
                                       ALU.add))

            def route_experts(link, b):
                dve.memset(carrier[:], 0.0)
                for t in range(T):
                    last = dve.max(top[:, t, :], cand[:, t, :])
                link(last)
                link(dve.memset(top[:, :, TOP_K:8], SENTINEL), apart=True)
                for t in range(T):
                    last = dve.match_replace(repl[:, t, :], top[:, t, :], cand[:, t, :], REPLACED)
                link(last)
                link(dve.tensor_tensor(chosen[:], repl[:, :, 0:E], cand[:, :, 0:E], ALU.not_equal))
                link(dve.tensor_tensor(chosen[:], chosen[:], cand[:, :, 0:E], ALU.mult))
                link(dve.tensor_reduce(den[:], chosen[:], AX.X, ALU.add))
                link(dve.tensor_scalar(den[:], den[:], 1e-20, None, ALU.add))
                link(dve.reciprocal(den[:], den[:]))
                link(dve.scalar_tensor_tensor(out=comb[:], in0=chosen[:], scalar=SCALE,
                                              in1=broadcast(den[:], [P, T, E], 2), op0=ALU.mult, op1=ALU.mult))
                split(link, cs, comb[:], c_ready)

            def step(s, q, on, at):
                pq = 1 - q
                O, F = "O" in on, "F" in on
                b, fb = s - 1, s - 2
                if O:
                    link_o = Chain(ch_o, O_OPS, b)
                if F:
                    link_f = Chain(ch_f, F_OPS, fb)

                def gate_up(cs):
                    for c in cs:
                        dve.wait_ge(silu_done, FC * fb + c + 1)
                        if c == 0:
                            wait(dve, done["y2"], 2 * fb)
                        dve.tensor_tensor(it[:, c, :], bank[("gu", c)][:, N:2 * N], sg[c % 2][:], ALU.mult)\
                           .then_inc(read["gu"], 1)

                def scale_heads(js):
                    for j in js:
                        dve.wait_ge(done["rB"], 4 * b + j + 1)
                        dve.wait_ge(aw_done, 8 * b + 8)
                        part = aw[pq][:, 2 * j:2 * j + 2, :]
                        dve.tensor_tensor(part, bank[("rB", j)][:].rearrange("p (c n) -> p c n", n=N), part, ALU.mult)\
                           .then_inc(read["rB"], 1)

                L_on, P_on = "L" in on, "P" in on
                if L_on:
                    link_l = Chain(ch_l, 3, s + 2)
                if P_on:
                    link_p = Chain(ch_p, P_OPS, s + 1)
                if O:
                    link_n = Chain(ch_n, 3, b)
                if P_on or O:
                    link_norms = Chain(ch_norms, NORM_OPS, s + 1)
                if L_on or O:
                    link_ln = Chain(ch_ln, LN_OPS, s + 2)

                for k in range(SLOTS):
                    if ("A" in on and k > 0) or (O and k == 0):
                        pair, ab, ap = (k - 1, s, q) if k > 0 else (NP - 1, b, pq)
                        dve.wait_ge(a2_done, 8 * ab + pair + 1)
                        dve.wait_ge(gate_ready, 4 * ab + pair // 2 + 1)
                        if pair == 0:
                            wait(dve, done["y"], 2 * (s - 1))
                        dve.tensor_tensor(aw[ap][:, pair, :], ps_a[pair % 2][:, 0:N], wt[ap][:, pair, :], ALU.mult)\
                           .then_inc(aw_done, 1)
                    if k == 0:
                        if P_on:
                            for j in range(4):
                                sums(j, s + 1)
                    if k == 1:
                        if P_on:
                            for j in range(4, 6):
                                sums(j, s + 1)
                        if O:
                            dve.wait_ge(done["nT"], b + 1)
                            dve.tensor_copy(n2, bank[("nT", 0)][:, 0:T * H]).then_inc(read["nT"], 1)
                        if F:
                            gate_up([0])
                        if P_on or O:
                            norms_start(link_norms, P_on, O, s)
                        if F:
                            gate_up([1, 2])
                    if k == 2:
                        for c in range(3):
                            if P_on or O:
                                newton(link_norms, nt)
                            if F:
                                gate_up([3 + c])
                        if O:
                            head_norms(link_o, b, rq2[pq])
                        if F:
                            gate_up([6])
                    if k == 3:
                        if P_on:
                            value_scales(link_p, s + 1, rq2[pq])
                            link_p.end()
                        if F:
                            gate_up([7])
                        if O:
                            head_scales(link_o, b)
                            link_o.end()
                        if F:
                            gate_up([8])
                            route_groups(link_f, fb)
                    if k == 4:
                        if O:
                            scale_heads([0, 1, 2, 3])
                        if L_on:
                            dve.wait_ge(x_loaded[q], (s + 2 - q) * 8 + 16)
                            row_stats(link_l, x_in[q], st1, mv1, 0)
                            link_l.end()
                    if k == 5:
                        if F:
                            route_experts(link_f, fb)
                            link_f.end()
                    if k == 6:
                        if O:
                            dve.wait_ge(x_kept, b + 1)
                            for t in range(T):
                                dve.wait_ge(done["y"], 2 * b + t + 1)
                                dve.tensor_tensor(x1[pq][:, t, :], bank[("y", t)][:, 0:D], x_res[pq][:, t, :], ALU.add)\
                                   .then_inc(read["y"], 1)
                            dve.wait_ge(read["y"], 2 * b + 2)
                            row_stats(link_n, x1[pq], st2, mv2, 1)
                            link_n.end()
                        if L_on or O:
                            seed(link_ln, ln)
                        for j in range(4):
                            if F:
                                if j == 0:
                                    dve.wait_ge(read["gu"], FC * fb + FC)
                                dve.wait_ge(done["cB"], 4 * fb + j + 1)
                                part = it[:, 2 * j:2 * j + 2, :]
                                dve.tensor_tensor(part, bank[("cB", j)][:].rearrange("p (c n) -> p c n", n=N), part,
                                                  ALU.mult).then_inc(read["cB"], 1)
                            if j < 3 and (L_on or O):
                                newton(link_ln, ln)
                    if k == 7:
                        if O:
                            wait(dve, done["x2T"], b)
                            normed_rows(x1[pq], mv2, 1, xn2, ln2_ready)
                        if L_on:
                            wait(dve, done["xT"], s + 2)
                            normed_rows(x_in[q], mv1, 0, xn, ln1_ready)
                        if at == FIRST_STEP:
                            projection_weights()
                        if P_on:
                            wait(dve, read["y"], 2 * s)
                            dve.wait_ge(x_loaded[pq], (s + 1 - pq) * 8 + 16)
                            dve.tensor_copy(x_res[pq][:], x_in[pq][:]).then_inc(x_kept, 1)
                        if O:
                            dve.wait_ge(x2h_ready, b + 1)
                            dve.tensor_tensor(x2l[:], bank[("x2T", 0)][:, 0:N], x2h[:].bitcast(F32), ALU.subtract)\
                               .then_inc(read["x2T"], 1)
                        if L_on:
                            dve.wait_ge(xh_ready, s + 3)
                            dve.tensor_tensor(xl[:], bank[("xT", 0)][:, 0:N], xh[:].bitcast(F32), ALU.subtract)\
                               .then_inc(read["xT"], 1)
                        if at == -1:
                            expert_weights()
                            dve.wait_ge(w_lo, 7)
                        if F:
                            wait(dve, out_stored, 16 * fb)
                            for t in range(T):
                                dve.wait_ge(done["y2"], 2 * fb + t + 1)
                                dve.tensor_tensor(o_sb[:, t, :], bank[("y2", t)][:, 0:D], x1[q][:, t, :], ALU.add)\
                                   .then_inc(read["y2"], 1)

            run_steps(dve, step)


_INS = ["L0_attn_tokens", "L0_attn_Wqg", "L0_attn_Wkv", "L0_attn_Wout", "L0_ffn_gate_kernel", "L0_ffn_gate_bias",
        "L0_ffn_w_gate", "L0_ffn_w_up", "L0_ffn_w_down", "L0_ffn_sw_gate", "L0_ffn_sw_up", "L0_ffn_sw_down"]


def kernel(**inputs):
    import numpy as np
    import concourse.bacc as bacc
    from concourse.bass_utils import run_bass_kernel_spmd

    nc = bacc.Bacc("TRN2", target_bir_lowering=False, num_devices=1)
    arrays, args = {}, []
    for name in _INS:
        a = np.ascontiguousarray(inputs[name])
        arrays[f"in_{name}"] = a
        args.append(nc.dram_tensor(f"in_{name}", a.shape, mybir.dt.from_np(a.dtype), kind="ExternalInput").ap())
    shape = inputs["L0_attn_tokens"].shape
    args.append(nc.dram_tensor("out_0", shape, F32, kind="ExternalOutput").ap())
    bass_attn_moe_layer_kernel(nc, *args)
    result = run_bass_kernel_spmd(nc, [arrays], core_ids=[0])
    return result.results[0]["out_0"]
```

```python
from contextlib import ExitStack

import concourse.bass as bass
from concourse import mybir

F32 = mybir.dt.float32
F32R = mybir.dt.float32r
I32 = mybir.dt.int32
ALU = mybir.AluOpType
ACT = mybir.ActivationFunctionType
AX = mybir.AxisListType

P = 128
EPS_LN = 1e-5
INV_EPS = 1e12
RSQRT_MAGIC = 1597463007.0
SCALE = 2.5
SENTINEL = -2.0e38


def bass_attn_moe_layer_kernel(nc, tokens, Wqg, Wkv, Wout, gate_kernel, gate_bias,
                               w_gate, w_up, w_down, sw_gate, sw_up, sw_down, out):
    B, N, D = tokens.shape
    E, _, M = w_gate.shape
    T = N // P
    DV = 64
    H = Wout.shape[0] // DV
    DK = Wqg.shape[1] // H - DV
    NP = H // 2
    EC = E // 2
    FC = EC + 1
    NG = 4
    EG = E // NG
    TOP_K = 4
    HK = H * DK
    HV = H * DV
    SLOTS = NP
    assert D == P and T == 2 and DK == 16 and 2 * M == P and 2 * DV == P and H == E == 16 and FC == 9

    SKIP = ("-", "skip", 0)
    FILL = [
        [("P", "qk", 0), ("P", "qk", 1), ("P", "v", 0), ("O", "ones", 0), ("P", "v", 1), ("P", "v", 2)],
        [("F", "gu", 0), ("P", "v", 3), ("O", "nT", 0), ("F", "lg", 0), ("F", "gu", 1), ("F", "gu", 2)],
        [("F", "gu", 3), ("F", "gu", 4), ("F", "gu", 5), ("F", "gu", 6), ("F", "gu", 7)],
        [("P", "g", 0), ("P", "g", 1), ("F", "gu", 8), ("P", "g", 2), ("O", "rT", 0)],
        [("O", "rB", 0), ("P", "g", 3), ("O", "rB", 1), ("P", "tr", 0), ("O", "rB", 2), ("P", "tr", 1), ("O", "rB", 3),
         ("P", "tr", 2)],
        [("O", "y", 0), ("O", "y", 1), ("P", "tr", 3), ("F", "cT", 0), SKIP],
        [("F", "cB", 0), ("P", "tr", 4), ("F", "cB", 1), ("P", "tr", 5), ("F", "cB", 2), ("P", "tr", 6), ("F", "cB", 3),
         ("P", "tr", 7), SKIP],
        [("F", "y2", 0), ("O", "x2T", 0), ("L", "xT", 0), ("F", "y2", 1)],
    ]
    ORDER = [job for slot in FILL for job in slot]
    assert len(FILL) == SLOTS and len(ORDER) % 4 == 0
    OFFSET = {"L": 2, "P": 1, "A": 0, "O": -1, "F": -2}
    JOBS = {"xT": 1, "qk": 2, "v": 4, "g": 4, "tr": NP, "ones": 1, "nT": 1, "rT": 1, "rB": 4, "y": 2,
            "x2T": 1, "lg": 1, "gu": FC, "cT": 1, "cB": 4, "y2": 2}

    def stages(s):
        return {k for k, d in OFFSET.items() if 0 <= s + d < B}

    ALL = set(OFFSET)
    FIRST_STEP, LOOP_FROM, LOOP_TO, LAST_STEP = -2, 4, B - 2, B + 1
    assert all(stages(s) == ALL for s in range(LOOP_FROM - 1, LOOP_TO)) and (LOOP_TO - LOOP_FROM) % 2 == 0

    with ExitStack() as ctx:
        def sb(name, shape, dt=F32):
            return ctx.enter_context(nc.sbuf_tensor(name, shape, dt))

        def sem(name):
            return ctx.enter_context(nc.semaphore(name))

        wqk = [sb(f"wqk_{k}", [P, 2 * HK], F32R) for k in ("hi", "lo")]
        wv = [sb(f"wv_{k}", [P, HV], F32R) for k in ("hi", "lo")]
        wg = [sb(f"wg_{k}", [P, HV], F32R) for k in ("hi", "lo")]
        weg = [sb(f"weg_{k}", [P, FC * P], F32R) for k in ("hi", "lo")]
        weu = [sb(f"weu_{k}", [P, FC * P], F32R) for k in ("hi", "lo")]
        wout = sb("wout", [P, NP, D])
        wdown = sb("wdown", [P, FC, D])
        wroute = sb("wroute", [P, E])
        bias = sb("bias", [P, E])
        ident = sb("ident", [P, P])
        ones32 = sb("ones32", [P, 2, 32])
        pick = sb("pick", [P, H])
        sel = sb("sel", [2 * H, NP, P], F32R)
        lower = sb("lower", [P, NG, NG])
        RAW = 2 * (HK + HV) + 2 * FC * P
        big = sb("big", [P, max(RAW, 3 * NP * N)])
        a2 = big[:, 0:NP * N].rearrange("p (c n) -> p c n", n=N)
        aw = [big[:, q * NP * N:(q + 1) * NP * N].rearrange("p (c n) -> p c n", n=N) for q in (1, 2)]
        raw_experts = 3 * NP * N - 2 * FC * P
        assert 2 * (HK + HV) <= raw_experts and 2 * NP * N - N <= raw_experts
        x_in = [sb(f"x_in{q}", [P, T, D]) for q in range(2)]
        x_res = [sb(f"x_res{q}", [P, T, D]) for q in range(2)]
        xn = sb("xn", [P, T, D])
        xh, xl = sb("xh", [P, N], F32R), sb("xl", [P, N], F32R)
        qk = sb("qk", [P, T, 2 * HK])
        qks = sb("qks", [P, T, 2 * H, 4, DK], F32R)
        qkt = [sb(f"qkt{q}", [P, NP, 2 * N], F32R) for q in range(2)]
        v = [sb(f"v{q}", [P, T, HV]) for q in range(2)]
        wt = [sb(f"wt{q}", [P, NP, N]) for q in range(2)]
        r = [sb(f"r{k}", [P, 2 * N]) for k in range(2)]
        p = [sb(f"p{k}", [P, 2 * N]) for k in range(4)]
        rs = sb("rs", [P, T, 2, H])
        rt = sb("rt", [2 * H, N], F32R)
        sq = sb("sq", [P, 4 * 512])
        selraw = sq[0:2 * H, 0:NP * P].rearrange("p (c n) -> p c n", n=P)
        x1 = [sb(f"x1_{q}", [P, T, D]) for q in range(2)]
        n2row = [x1[q][:].rearrange("p t d -> p (t d)") for q in range(2)]
        xn2 = sb("xn2", [P, T, D])
        x2t = xn2[:].rearrange("p t d -> p (t d)")
        x2h, x2l = sb("x2h", [P, N], F32R), sb("x2l", [P, N], F32R)
        it = sb("it", [P, FC, N])
        cs = sb("cs", [P, T, 2, E])
        o_sb = sb("o_sb", [P, T, D])

        def norm_tiles(name, n):
            return {k: sb(f"{name}_{k}", [P, n]) for k in ("m", "y", "t")}

        st1, mv1 = sb("st1", [P, T, 6]), sb("mv1", [P, T, 2])
        st2, mv2 = sb("st2", [P, T, 6]), sb("mv2", [P, T, 2])
        ln = norm_tiles("ln", 2 * T)
        S3 = 2 * H + H
        NS = T * S3
        nt = norm_tiles("norms", NS + T * H)
        ss = nt["m"]
        ss3 = ss[:, 0:NS].rearrange("p (t h) -> p t h", t=T)
        rn3 = nt["y"][:, 0:NS].rearrange("p (t h) -> p t h", t=T)
        n2, rn2 = ss[:, NS:], nt["y"][:, NS:]
        rk2, vs = sb("rk2", [P, T, H]), sb("vs", [P, T, H])
        rq2 = [sb(f"rq2_{q}", [P, T, H]) for q in range(2)]
        nn, bound = sb("nn", [P, T * H]), sb("bound", [P, T * H])
        th, sc = sb("th", [P, T * E]), sb("sc", [P, T * E])
        pairs, gsum = sb("pairs", [P, T * NG, 6]), sb("gsum", [P, T * NG])
        gt, eq = sb("gt", [P, T, NG, NG]), sb("eq", [P, T, NG, NG])
        rank = sb("rank", [P, T * NG])
        EB = E + 8
        cand, repl = sb("cand", [P, T, EB]), sb("repl", [P, T, EB])
        top = sb("top", [P, T, 8])
        chosen = sb("chosen", [P, T, E])
        den, comb = sb("den", [P, T]), sb("comb", [P, T, E])
        split_hi = sb("split_hi", [P, T, H], F32R)
        carrier = sb("carrier", [P, 1])

        ps_s = [ctx.enter_context(nc.psum_tensor(f"ps_s{k}", [P, 512], F32)) for k in range(2)]
        ps_a = [ctx.enter_context(nc.psum_tensor(f"ps_a{k}", [P, 512], F32)) for k in range(2)]
        ps_f = [ctx.enter_context(nc.psum_tensor(f"ps_f{k}", [P, 512], F32)) for k in range(4)]
        bank = {job[1:]: ps_f[n % 4] for n, job in enumerate(ORDER) if job != SKIP}

        x_loaded = [sem(f"x_loaded{q}") for q in range(2)]
        w_loaded = [sem(f"w_loaded{k}") for k in range(3)]
        c_loaded = sem("c_loaded")
        out_stored = sem("out_stored")
        consts_pool, consts_dve = sem("consts_pool"), sem("consts_dve")
        w_hi, w_lo = sem("w_hi"), sem("w_lo")
        done = {k: sem(f"{k}_done") for k in JOBS}
        read = {k: sem(f"{k}_read") for k in JOBS}
        scores_done, values_done = sem("scores_done"), sem("values_done")
        relu_done, probs_done = sem("relu_done"), sem("probs_done")
        a2_done, aw_done = sem("a2_done"), sem("aw_done")
        ln1_ready, xh_ready, x_kept = sem("ln1_ready"), sem("xh_ready"), sem("x_kept")
        squares_done = sem("squares_done")
        sums_done, vs_ready, v_normed = sem("sums_done"), sem("vs_ready"), sem("v_normed")
        qk_hi, qk_lo = [sem(f"qk_hi{t}") for t in range(T)], sem("qk_lo")
        gate_ready = sem("gate_ready")
        n_ready, tanh_n, r_ready = sem("n_ready"), sem("tanh_n"), sem("r_ready")
        ln2_ready, x2h_ready = sem("ln2_ready"), sem("x2h_ready")
        silu_done, c_ready = sem("silu_done"), sem("c_ready")
        ch_l, ch_p, ch_o, ch_n, ch_f = (sem(f"ch_{k}") for k in "lponf")
        ch_norms, ch_ln = sem("ch_norms"), sem("ch_ln")

        block = ctx.enter_context(nc.Block())

        def run_steps(eng, step):
            for s in range(FIRST_STEP, LOOP_FROM):
                step(s, s % 2, stages(s), s)
            with eng.Fori(LOOP_FROM // 2, LOOP_TO // 2) as i:
                step(i * 2, 0, ALL, None)
                step(i * 2 + 1, 1, ALL, None)
            for s in range(LOOP_TO, LAST_STEP + 1):
                step(s, s % 2, stages(s), s)

        def wait(eng, semaphore, value):
            if not isinstance(value, int) or value > 0:
                eng.wait_ge(semaphore, value)

        def at_most(value, most):
            return min(value, most) if isinstance(value, int) else value

        def broadcast(ap, shape, at):
            return ap.unsqueeze(at).broadcast_to(shape)

        def squares_at(j):
            return sq[:, (j % 4) * 512:(j % 4 + 1) * 512]

        def slots_of(part, t):
            heads = qks[:, t, H * part:H * part + H, :, :]
            if part == 0:
                heads = heads.rearrange("p h (r a) d -> p a h r d", a=2)
            else:
                heads = heads.rearrange("p h (a r) d -> p a h r d", a=2)
            whole = qk[:, t, HK * part:HK * part + HK].rearrange("p (h d) -> p h d", d=DK)
            return heads[:, 0], heads[:, 1], broadcast(whole, [P, H, 2, DK], 2)

        @block.sync
        def _(sp):
            def load_x(b, q):
                sp.dma_start(x_in[q][:], tokens[b].rearrange("(t p) d -> p t d", p=P)).then_inc(x_loaded[q], 16)

            load_x(0, 0)
            sp.dma_start(big[:, 0:HK + HV], Wqg).then_inc(w_loaded[0], 16)
            sp.dma_start(big[:, HK + HV:2 * (HK + HV)], Wkv).then_inc(w_loaded[0], 16)
            load_x(1, 1)
            base = raw_experts
            for w, sw in ((w_gate, sw_gate), (w_up, sw_up)):
                k = 1 if w is w_gate else 2
                sp.dma_start(big[:, base:base + E * M].rearrange("p (e m) -> p e m", m=M),
                             w.rearrange("e h m -> h e m")).then_inc(w_loaded[k], 16)
                sp.dma_start(big[:, base + E * M:base + FC * P], sw).then_inc(w_loaded[k], 16)
                base += FC * P
            sp.dma_start(wout[:], Wout.rearrange("(c p) n -> p c n", p=P)).then_inc(c_loaded, 16)
            sp.dma_start(wdown[:, 0:EC, :], w_down.rearrange("(c e) m h -> (e m) c h", e=2)).then_inc(c_loaded, 16)
            sp.dma_start(wdown[:, EC, :], sw_down).then_inc(c_loaded, 16)
            sp.dma_start(wroute[:], gate_kernel).then_inc(c_loaded, 16)
            sp.dma_start(bias[:], gate_bias.rearrange("(a e) -> a e", a=1).broadcast_to([P, E])).then_inc(c_loaded, 16)

            def step(s, q, on, at):
                if "L" in on and "A" in on:
                    sp.wait_ge(x_kept, s + 1)
                    sp.wait_ge(ln1_ready, s + 1)
                    load_x(s + 2, q)
                if "F" in on:
                    sp.wait_ge(read["y2"], (s - 1) * 2)
                    sp.dma_start(out[s - 2].rearrange("(t p) d -> p t d", p=P), o_sb[:])\
                      .then_inc(out_stored, 16)

            run_steps(sp, step)
            sp.wait_ge(out_stored, 16 * B)

        @block.gpsimd
        def _(pool):
            n = [0]

            def built(ins):
                n[0] += 1
                ins.then_inc(consts_pool, 1)
                pool.wait_ge(consts_pool, n[0])

            built(pool.memset(ident[:], 0.0))
            built(pool.affine_select(out=ident[:], in_=ident[:], compare_op=ALU.not_equal, fill=1.0, base=0,
                                     pattern=[[-1, P]], channel_multiplier=1))
            built(pool.memset(selraw, 0.0))
            for part in range(2):
                view = selraw.rearrange("k c (e m) -> k c e m", e=2)
                built(pool.affine_select(out=view, in_=view, compare_op=ALU.not_equal, fill=1.0, base=-H * part,
                                         pattern=[[-2, NP], [-1, 2], [0, DV]], channel_multiplier=1))
            built(pool.memset(pick[:], 0.0))
            view = pick[:].rearrange("p (a j e) -> p a j e", j=4, e=2)
            built(pool.affine_select(out=view, in_=view, compare_op=ALU.not_equal, fill=1.0, base=0,
                                     pattern=[[-2, 2], [-32, 4], [-1, 2]], channel_multiplier=1))

            def step(s, q, on, at):
                for k in range(SLOTS):
                    if "A" in on:
                        for h in (2 * k, 2 * k + 1):
                            wait(pool, values_done, 8 * s + (h - 4) // 2 + 1)
                            pool.wait_ge(relu_done, 16 * s + h + 1)
                            pool.tensor_tensor(p[h % 4][:], r[h % 2][:], r[h % 2][:], ALU.mult).then_inc(probs_done, 1)
                    if "P" in on:
                        b = s + 1
                        if k in (1, 2):
                            t = k - 1
                            wait(pool, done["tr"], 8 * b)
                            for part in range(2):
                                pool.wait_ge(qk_hi[t], 2 * b + part + 1)
                                hi, lo, whole = slots_of(part, t)
                                pool.tensor_tensor(lo, whole, hi.bitcast(F32), ALU.subtract).then_inc(qk_lo, 1)
                        if k in (4, 5, 6, 7):
                            t, half = divmod(k - 4, 2)
                            pool.wait_ge(vs_ready, b + 1)
                            pool.wait_ge(read["v"], 4 * b + k - 3)
                            view = v[1 - q][:, t, half * 512:(half + 1) * 512].rearrange("p (h d) -> p h d", d=DV)
                            scale = vs[:, t, half * NP:(half + 1) * NP]
                            pool.tensor_tensor(view, view, broadcast(scale, [P, NP, DV], 2), ALU.mult)\
                                .then_inc(v_normed, 1)

            run_steps(pool, step)

        @block.tensor
        def _(pe):
            pe.wait_ge(consts_pool, 7)
            pe.wait_ge(consts_dve, 2)
            weights = {"qk": 2, "v": 3, "g": 4, "gu": 6, "lg": 7, "y": 7, "y2": 7}

            def three(dst, stat, mov):
                pe.matmul(dst, stat[0], mov[0], start=True, stop=False)
                pe.matmul(dst, stat[0], mov[1], start=False, stop=False)
                return pe.matmul(dst, stat[1], mov[0], start=False, stop=True)

            def filler(stage, kind, j, s, q, at):
                b = s + OFFSET[stage]
                ps = bank[(kind, j)]
                pb = 1 - q
                if at is not None and kind in weights:
                    pe.wait_ge(w_lo, weights[kind])
                tok = [slice(t * P, (t + 1) * P) for t in range(T)]
                if kind == "xT":
                    pe.wait_ge(ln1_ready, b + 1)
                    for t in range(T):
                        last = pe.transpose(ps[:, tok[t]], xn[:, t, :], ident[:])
                elif kind == "qk":
                    if j == 0:
                        pe.wait_ge(xh_ready, b + 1)
                        pe.wait_ge(read["xT"], b + 1)
                    last = three(ps[:, 0:2 * HK], (xh[:, tok[j]], xl[:, tok[j]]), (wqk[0][:], wqk[1][:]))
                elif kind == "v":
                    half = slice((j % 2) * 512, (j % 2 + 1) * 512)
                    last = three(ps[:, :], (xh[:, tok[j // 2]], xl[:, tok[j // 2]]), (wv[0][:, half], wv[1][:, half]))
                elif kind == "g":
                    for c in range(2):
                        cols = slice((2 * j + c) * P, (2 * j + c + 1) * P)
                        last = three(ps[:, c * N:(c + 1) * N], (wg[0][:, cols], wg[1][:, cols]), (xh[:], xl[:]))
                elif kind == "tr":
                    if j == 0:
                        pe.wait_ge(qk_lo, 4 * b + 4)
                    for part in range(2):
                        for t in range(T):
                            src = qks[:, t, H * part + 2 * j:H * part + 2 * j + 2, :, :].bitcast(F32)
                            src = src.rearrange("p h a d -> p (h a d)")
                            last = pe.transpose(ps[:, part * N + t * P:part * N + (t + 1) * P], src, ident[:])
                elif kind == "ones":
                    pe.wait_ge(a2_done, 8 * b + 8)
                    for a in range(2):
                        for c in range(4):
                            last = pe.matmul(ps[32 * c:32 * c + 32, 0:N], ones32[:, a, :], a2[:, 4 * a + c, :],
                                             start=(a == 0), stop=(a == 1))
                elif kind == "nT":
                    pe.wait_ge(read["ones"], b + 1)
                    for t in range(T):
                        last = pe.matmul(ps[:, t * H:(t + 1) * H], n2row[pb][:, tok[t]], pick[:], start=True, stop=True)
                elif kind in ("rT", "cT"):
                    pe.wait_ge(r_ready if kind == "rT" else c_ready, b + 1)
                    src = rs if kind == "rT" else cs
                    for t in range(T):
                        last = pe.transpose(ps[0:2 * H, tok[t]], src[:, t, :, :].rearrange("p a h -> p (a h)"), ident[:])
                elif kind in ("rB", "cB"):
                    ready = read["rT" if kind == "rB" else "cT"]
                    if j == 0:
                        pe.wait_ge(ready, b + 1)
                    for c in range(2):
                        last = pe.matmul(ps[:, c * N:(c + 1) * N], sel[:, 2 * j + c, :], rt[:], start=True, stop=True)
                elif kind == "y":
                    pe.wait_ge(read["rB"], 4 * b + 4)
                    for c in range(NP):
                        last = pe.matmul(ps[:, 0:D], aw[pb][:, c, tok[j]], wout[:, c, :],
                                         start=(c == 0), stop=(c == NP - 1))
                elif kind == "x2T":
                    pe.wait_ge(ln2_ready, b + 1)
                    for t in range(T):
                        last = pe.transpose(ps[:, tok[t]], xn2[:, t, :], ident[:])
                elif kind == "lg":
                    for t in range(T):
                        last = pe.matmul(ps[:, t * E:(t + 1) * E], x2t[:, tok[t]], wroute[:], start=True, stop=True)
                elif kind == "gu":
                    if j == 0:
                        pe.wait_ge(x2h_ready, b + 1)
                        pe.wait_ge(read["x2T"], b + 1)
                    cols = slice(j * P, (j + 1) * P)
                    three(ps[:, 0:N], (weg[0][:, cols], weg[1][:, cols]), (x2h[:], x2l[:]))
                    last = three(ps[:, N:2 * N], (weu[0][:, cols], weu[1][:, cols]), (x2h[:], x2l[:]))
                else:
                    pe.wait_ge(read["cB"], 4 * b + 4)
                    for c in range(FC):
                        last = pe.matmul(ps[:, 0:D], it[:, c, tok[j]], wdown[:, c, :],
                                         start=(c == 0), stop=(c == FC - 1))
                last.then_inc(done[kind], 1)

            def wait_for_bank(n, s, at):
                m, d = n - 4, 0
                while True:
                    if m < 0:
                        m, d = m + len(ORDER), d - 1
                    stage, kind, j = ORDER[m]
                    if stage in (ALL if at is None else stages(at + d)):
                        break
                    if at is not None and at + d < FIRST_STEP:
                        return
                    m -= 4
                wait(pe, read[kind], (s + d + OFFSET[stage]) * JOBS[kind] + j + 1)

            def scores(b, q, k):
                if k == 0:
                    pe.wait_ge(read["tr"], 8 * b + 8)
                for t in range(T):
                    for e in range(2):
                        if t == 0:
                            wait(pe, relu_done, 16 * b + 2 * k + e - 1)
                        rows = slice(64 * e, 64 * e + 64)
                        last = pe.matmul(ps_s[e][:, t * N:(t + 1) * N],
                                         qkt[q][rows, k, N + t * P:N + (t + 1) * P], qkt[q][rows, k, 0:N],
                                         start=True, stop=True)
                        if t == T - 1:
                            last.then_inc(scores_done, 1)

            def step(s, q, on, at):
                n = 0
                for k in range(SLOTS):
                    for stage, kind, j in FILL[k]:
                        if stage in on:
                            wait_for_bank(n, s, at)
                            filler(stage, kind, j, s, q, at)
                        n += 1
                    if k < SLOTS - 1:
                        if "A" in on:
                            scores(s, q, k + 1)
                    elif at is None or "A" in stages(at + 1):
                        scores(s + 1, 1 - q, 0)
                    if "A" in on:
                        wait(pe, aw_done, 8 * s + k - 1)
                        if k == 0:
                            pe.wait_ge(v_normed, 4 * s + 4)
                        for t in range(T):
                            for e in range(2):
                                h = 2 * k + e
                                if t == 0:
                                    pe.wait_ge(probs_done, 16 * s + h + 1)
                                last = pe.matmul(ps_a[k % 2][64 * e:64 * e + 64, 0:N],
                                                 v[q][:, t, h * DV:(h + 1) * DV], p[h % 4][:, t * N:(t + 1) * N],
                                                 start=(t == 0), stop=(t == T - 1))
                        last.then_inc(values_done, 1)

            run_steps(pe, step)

        @block.scalar
        def _(act):
            act.wait_ge(consts_pool, 2)
            act.activation(it[0:1, 0, 0:1], ident[0:1, 0:1], ACT.Silu)
            act.wait_ge(w_loaded[0], 32)
            gq = big[:, 0:HK + HV].rearrange("p (h c) -> p h c", h=H)
            kv = big[:, HK + HV:2 * (HK + HV)].rearrange("p (h c) -> p h c", h=H)
            base = raw_experts

            def heads(w, c):
                return w.rearrange("p (h c) -> p h c", c=c)

            act.activation(heads(wqk[0][:, 0:HK], DK), gq[:, :, 0:DK], ACT.Copy).then_inc(w_hi, 1)
            act.activation(heads(wqk[0][:, HK:2 * HK], DK), kv[:, :, 0:DK], ACT.Copy).then_inc(w_hi, 1)
            act.activation(heads(wv[0][:], DV), kv[:, :, DK:], ACT.Copy).then_inc(w_hi, 1)
            act.activation(heads(wg[0][:], DV), gq[:, :, DK:], ACT.Copy).then_inc(w_hi, 1)
            act.wait_ge(consts_dve, 2)

            def expert_weights():
                act.wait_ge(w_loaded[1], 32)
                act.activation(weg[0][:], big[:, base:base + FC * P], ACT.Copy).then_inc(w_hi, 1)
                act.wait_ge(w_loaded[2], 32)
                act.activation(weu[0][:], big[:, base + FC * P:base + 2 * FC * P], ACT.Copy).then_inc(w_hi, 1)

            def high_parts(t, s):
                b = s + 1
                wait(act, done["tr"], 8 * b)
                act.wait_ge(read["qk"], 2 * b + t + 1)
                for part in range(2):
                    hi, _, whole = slots_of(part, t)
                    act.activation(hi, whole, ACT.Copy).then_inc(qk_hi[t], 1)

            def gates(j, s, q):
                b = s + 1
                dst = wt[1 - q][:, 2 * j:2 * j + 2, :]
                act.wait_ge(read["g"], 4 * b + j + 1)
                act.activation(dst, dst, ACT.Tanh).then_inc(gate_ready, 1)

            def evacuate(stage, kind, j, s, q):
                b = s + OFFSET[stage]
                pq = 1 - q
                ps = bank[(kind, j)]
                count = b * JOBS[kind] + j + 1
                if kind == "xT":
                    wait(act, done["g"], 4 * b)
                    act.wait_ge(done[kind], count)
                    act.activation(xh[:], ps[:, 0:N], ACT.Copy).then_inc(xh_ready, 1)
                elif kind == "qk":
                    wait(act, qk_lo, 4 * b)
                    act.wait_ge(done[kind], count)
                    act.activation(qk[:, j, :], ps[:, 0:2 * HK], ACT.Copy).then_inc(read[kind], 1)
                elif kind == "v":
                    if j == 0:
                        wait(act, values_done, 8 * (b - 1))
                    act.wait_ge(done[kind], count)
                    act.activation(v[pq][:, j // 2, (j % 2) * 512:(j % 2 + 1) * 512], ps[:], ACT.Copy)
                    wait(act, sums_done, 6 * b + j - 1)
                    act.activation(squares_at(j + 2), ps[:], ACT.Square).then_inc(read[kind], 1)
                elif kind == "g":
                    if j == 0:
                        wait(act, aw_done, 8 * (b - 1))
                    act.wait_ge(done[kind], count)
                    dst = wt[pq][:, 2 * j:2 * j + 2, :]
                    act.activation(dst, ps[:].rearrange("p (c n) -> p c n", n=N), ACT.Silu).then_inc(read[kind], 1)
                elif kind == "tr":
                    if j == 0:
                        wait(act, scores_done, 16 * (b - 1))
                    act.wait_ge(done[kind], count)
                    act.activation(qkt[pq][:, j, :], ps[:], ACT.Copy).then_inc(read[kind], 1)
                elif kind == "ones":
                    wait(act, read["y2"], 2 * (b - 1))
                    act.wait_ge(done[kind], count)
                    act.activation(n2row[pq], ps[:, 0:N], ACT.Copy).then_inc(read[kind], 1)
                elif kind in ("rT", "cT"):
                    if kind == "rT":
                        wait(act, done["cB"], 4 * (b - 1))
                    else:
                        act.wait_ge(done["rB"], at_most(4 * (b + 2), 4 * B))
                    act.wait_ge(done[kind], count)
                    act.activation(rt[:], ps[0:2 * H, 0:N], ACT.Copy).then_inc(read[kind], 1)
                elif kind == "x2T":
                    wait(act, done["gu"], FC * b)
                    act.wait_ge(done[kind], count)
                    act.activation(x2t, ps[:, 0:N], ACT.Copy)
                    act.activation(x2h[:], ps[:, 0:N], ACT.Copy).then_inc(x2h_ready, 1)
                elif kind == "lg":
                    act.wait_ge(done[kind], count)
                    act.activation(th[:], ps[:, 0:T * E], ACT.Tanh, scale=0.5).then_inc(read[kind], 1)
                elif kind == "gu":
                    if j == 0:
                        wait(act, done["y2"], 2 * b)
                    act.wait_ge(done[kind], count)
                    act.activation(it[:, j, :], ps[:, 0:N], ACT.Silu).then_inc(silu_done, 1)

            def step(s, q, on, at):
                for k in range(SLOTS):
                    if "A" in on:
                        for h in (2 * k, 2 * k + 1):
                            wait(act, probs_done, 16 * s + h - 1)
                            act.wait_ge(scores_done, 16 * s + h + 1)
                            act.activation(r[h % 2][:], ps_s[h % 2][:], ACT.Relu).then_inc(relu_done, 1)
                    if ("A" in on and k > 0) or ("O" in on and k == 0):
                        pair, b = (k - 1, s) if k > 0 else (NP - 1, s - 1)
                        if pair == 0:
                            wait(act, done["ones"], s)
                            if at == 0:
                                act.wait_ge(w_lo, 4)
                        act.wait_ge(values_done, 8 * b + pair + 1)
                        act.activation(a2[:, pair, :], ps_a[pair % 2][:, 0:N], ACT.Square).then_inc(a2_done, 1)
                    for stage, kind, j in FILL[k]:
                        if stage in on:
                            evacuate(stage, kind, j, s, q)
                        if (kind, j) == ("g", 0) and "O" in on:
                            act.wait_ge(n_ready, s)
                            act.activation(nn[:], nn[:], ACT.Tanh).then_inc(tanh_n, 1)
                        if (kind, j) == (("qk", 1) if at == -1 else ("gu", 1)) and "P" in on:
                            high_parts(1, s)
                    for stage, kind, j in FILL[k - 1] if k > 0 else ():
                        if kind == "g" and stage in on and at != -1:
                            gates(j, s, q)
                    if at == 0 and k == 5:
                        expert_weights()
                if at == -1:
                    for j in range(4):
                        gates(j, s, q)

            run_steps(act, step)

        @block.vector
        def _(dve):
            class Chain:

                def __init__(self, semaphore, per, b):
                    self.semaphore, self.per, self.b, self.n = semaphore, per, b, 0

                def __call__(self, ins, apart=False):
                    self.n += 1
                    assert self.n <= self.per
                    ins.then_inc(self.semaphore, 1)
                    dve.wait_ge(self.semaphore, self.b * self.per + self.n)
                    if apart:
                        dve.memset(carrier[:], 0.0)

                def end(self):
                    assert self.n == self.per, self.n

            def seed(link, tiles):
                m, y = tiles["m"][:], tiles["y"][:]
                link(dve.tensor_single_scalar(y.bitcast(I32), m.bitcast(I32), 1, ALU.logical_shift_right))
                link(dve.tensor_scalar(y.bitcast(I32), y.bitcast(I32), -1.0, RSQRT_MAGIC, ALU.mult, ALU.add))

            def newton(link, tiles):
                m, y, t = tiles["m"][:], tiles["y"][:], tiles["t"][:]
                link(dve.tensor_tensor(t, m, y, ALU.mult))
                link(dve.scalar_tensor_tensor(out=t, in0=t, scalar=-0.5, in1=y, op0=ALU.mult, op1=ALU.mult))
                link(dve.scalar_tensor_tensor(out=y, in0=t, scalar=1.5, in1=y, op0=ALU.add, op1=ALU.mult))

            RS_OPS = 11
            LN_OPS, NORM_OPS, P_OPS, O_OPS, F_OPS = RS_OPS, RS_OPS, 2, 4, 17

            def row_stats(link, x, st, mv, part):
                for t in range(T):
                    last = dve.bn_stats(st[:, t, :], x[:, t, :])
                link(last, apart=True)
                for t in range(T):
                    last = dve.bn_aggr(mv[:, t, :], st[:, t, :])
                link(last)
                link(dve.tensor_scalar(ln["m"][:, part * T:part * T + T], mv[:, :, 1], EPS_LN, None, ALU.add))

            def normed_rows(x, mv, part, dst, ready):
                for t in range(T):
                    last = dve.tensor_scalar(dst[:, t, :], x[:, t, :], mv[:, t, 0:1],
                                             ln["y"][:, part * T + t:part * T + t + 1], ALU.subtract, ALU.mult)
                last.then_inc(ready, 1)

            n = [0]

            def built(ins):
                n[0] += 1
                ins.then_inc(consts_dve, 1)
                dve.wait_ge(consts_dve, n[0])

            dve.wait_ge(consts_pool, 7)
            dve.tensor_copy(sel[:], selraw)
            dve.memset(ones32[:], 0.0)
            dve.memset(ss[:], 1.0)
            dve.memset(ln["m"][:], 1.0)
            dve.memset(lower[:], 0.0)
            built(dve.memset(cand[:], SENTINEL))
            for e in range(2):
                for a in range(2):
                    dve.memset(ones32[64 * e:64 * e + 64, a, 2 * a + e:2 * a + e + 1], 1.0)
            for g in range(1, NG):
                last = dve.memset(lower[:, g, 0:g], 1.0)
            built(last)

            gq = big[:, 0:HK + HV].rearrange("p (h c) -> p h c", h=H)
            kv = big[:, HK + HV:2 * (HK + HV)].rearrange("p (h c) -> p h c", h=H)
            base = raw_experts

            def rest(k, w, raw, c):
                dve.wait_ge(w_hi, k)
                lo, hi = w[1], w[0]
                if c:
                    lo, hi = lo.rearrange("p (h c) -> p h c", c=c), hi.rearrange("p (h c) -> p h c", c=c)
                dve.tensor_tensor(lo, raw, hi.bitcast(F32), ALU.subtract).then_inc(w_lo, 1)

            def projection_weights():
                rest(1, [w[:, 0:HK] for w in wqk], gq[:, :, 0:DK], DK)
                rest(2, [w[:, HK:2 * HK] for w in wqk], kv[:, :, 0:DK], DK)
                rest(3, [w[:] for w in wv], kv[:, :, DK:], DV)
                rest(4, [w[:] for w in wg], gq[:, :, DK:], DV)

            def expert_weights():
                rest(5, [w[:] for w in weg], big[:, base:base + FC * P], 0)
                rest(6, [w[:] for w in weu], big[:, base + FC * P:base + 2 * FC * P], 0)
                dve.wait_ge(c_loaded, 80)
                dve.tensor_scalar(bias[:], bias[:], 0.5, None, ALU.add).then_inc(w_lo, 1)

            def squares(b):
                for j in range(2):
                    dve.wait_ge(read["qk"], 2 * b + j + 1)
                    dve.tensor_tensor(squares_at(j), qk[:, j, :], qk[:, j, :], ALU.mult)\
                       .then_inc(squares_done, 1)

            def high_parts(t, b):
                wait(dve, done["tr"], 8 * b)
                for part in range(2):
                    hi, _, whole = slots_of(part, t)
                    dve.tensor_copy(hi, whole).then_inc(qk_hi[t], 1)

            def sums(j, b):
                if j < 2:
                    dve.wait_ge(squares_done, 2 * b + j + 1)
                    dst, d = ss3[:, j, 0:2 * H], DK
                else:
                    t, half = divmod(j - 2, 2)
                    dve.wait_ge(read["v"], 4 * b + j - 1)
                    dst, d = ss3[:, t, 2 * H + half * NP:2 * H + (half + 1) * NP], DV
                dve.tensor_reduce(dst, squares_at(j).rearrange("p (h d) -> p h d", d=d),
                                  AX.X, ALU.add).then_inc(sums_done, 1)

            def norms_start(link, P_on, O_on, s):
                if P_on:
                    dve.wait_ge(sums_done, 6 * s + 12)
                if O_on:
                    dve.wait_ge(read["nT"], s)
                seed(link, nt)

            def head_norms(link, b, c):
                c = c[:].rearrange("p t h -> p (t h)")
                link(dve.tensor_tensor(nn[:], n2, rn2, ALU.mult))
                dve.tensor_tensor(nn[:], nn[:], c, ALU.mult).then_inc(n_ready, 1)
                link(dve.scalar_tensor_tensor(out=bound[:], in0=c, scalar=INV_EPS, in1=rn2, op0=ALU.mult, op1=ALU.min))
                dve.wait_ge(n_ready, b + 1)

            def value_scales(link, b, c):
                link(dve.tensor_scalar(rn3, rn3, INV_EPS, None, ALU.min))
                dve.tensor_tensor(c[:], rn3[:, :, 0:H], rn3[:, :, 0:H], ALU.mult)
                link(dve.tensor_tensor(rk2[:], rn3[:, :, H:2 * H], rn3[:, :, H:2 * H], ALU.mult))
                wait(dve, v_normed, 4 * b)
                dve.tensor_tensor(vs[:], rn3[:, :, 2 * H:S3], rk2[:], ALU.mult).then_inc(vs_ready, 1)

            def head_scales(link, b):
                dve.wait_ge(tanh_n, b + 1)
                link(dve.tensor_tensor(nn[:], nn[:], bound[:], ALU.mult))
                split(link, rs, nn[:].rearrange("p (t h) -> p t h", t=T), r_ready)

            def split(link, dst, src, ready):
                link(dve.tensor_copy(split_hi[:], src))
                dve.tensor_copy(dst[:, :, 0, :], split_hi[:].bitcast(F32))
                dve.tensor_tensor(dst[:, :, 1, :], src, split_hi[:].bitcast(F32), ALU.subtract).then_inc(ready, 1)

            def route_scores(link, b):
                dve.wait_ge(read["lg"], b + 1)
                link(dve.scalar_tensor_tensor(out=sc[:].rearrange("p (t e) -> p t e", t=T),
                                              in0=th[:].rearrange("p (t e) -> p t e", t=T), scalar=0.5,
                                              in1=broadcast(bias[:], [P, T, E], 1), op0=ALU.mult, op1=ALU.add))
                s4 = sc[:].rearrange("p (g e) -> p g e", e=EG)
                dve.tensor_tensor(pairs[:, :, 0:3], s4[:, :, 0:3], s4[:, :, 1:4], ALU.add)
                dve.tensor_tensor(pairs[:, :, 3:5], s4[:, :, 0:2], s4[:, :, 2:4], ALU.add)
                link(dve.tensor_tensor(pairs[:, :, 5:6], s4[:, :, 0:1], s4[:, :, 3:4], ALU.add))
                link(dve.tensor_reduce(gsum[:], pairs[:], AX.X, ALU.max))

            def route_groups(link):
                s4 = sc[:].rearrange("p (g e) -> p g e", e=EG)
                gs = gsum[:].rearrange("p (t g) -> p t g", t=T)
                other, own = broadcast(gs, [P, T, NG, NG], 2), broadcast(gs, [P, T, NG, NG], 3)
                dve.tensor_tensor(gt[:], other, own, ALU.is_gt)
                link(dve.tensor_tensor(eq[:], other, own, ALU.is_equal))
                link(dve.tensor_tensor(eq[:], eq[:], broadcast(lower[:], [P, T, NG, NG], 1), ALU.mult))
                link(dve.tensor_tensor(gt[:], gt[:], eq[:], ALU.add))
                link(dve.tensor_reduce(rank[:].rearrange("p (t g) -> p t g", t=T), gt[:], AX.X, ALU.add))
                for t in range(T):
                    out = cand[:, t, 0:E].rearrange("p (g e) -> p g e", e=EG)
                    kept = broadcast(rank[:, t * NG:(t + 1) * NG], [P, NG, EG], 2)
                    last = dve.scalar_tensor_tensor(out=out, in0=kept, scalar=2.0, in1=s4[:, t * NG:(t + 1) * NG, :],
                                                    op0=ALU.is_lt, op1=ALU.mult)
                link(last)

            def route_experts(link, b):
                dve.memset(carrier[:], 0.0)
                for t in range(T):
                    last = dve.max(top[:, t, :], cand[:, t, :])
                link(last)
                link(dve.memset(top[:, :, TOP_K:8], SENTINEL), apart=True)
                for t in range(T):
                    last = dve.match_replace(repl[:, t, :], top[:, t, :], cand[:, t, :], 0.0)
                link(last)
                link(dve.tensor_tensor(chosen[:], cand[:, :, 0:E], repl[:, :, 0:E], ALU.subtract))
                link(dve.tensor_reduce(den[:], chosen[:], AX.X, ALU.add))
                link(dve.tensor_scalar(den[:], den[:], 1e-20, None, ALU.add))
                link(dve.reciprocal(den[:], den[:]))
                link(dve.scalar_tensor_tensor(out=comb[:], in0=chosen[:], scalar=SCALE,
                                              in1=broadcast(den[:], [P, T, E], 2), op0=ALU.mult, op1=ALU.mult))
                split(link, cs, comb[:], c_ready)

            def step(s, q, on, at):
                pq = 1 - q
                O, F = "O" in on, "F" in on
                b, fb = s - 1, s - 2
                if O:
                    link_o = Chain(ch_o, O_OPS, b)
                if F:
                    link_f = Chain(ch_f, F_OPS, fb)

                def gate_up(cs):
                    for c in cs:
                        dve.wait_ge(silu_done, FC * fb + c + 1)
                        dve.tensor_tensor(it[:, c, :], bank[("gu", c)][:, N:2 * N], it[:, c, :], ALU.mult)\
                           .then_inc(read["gu"], 1)

                def scale_heads(js):
                    for j in js:
                        dve.wait_ge(done["rB"], 4 * b + j + 1)
                        dve.wait_ge(aw_done, 8 * b + 8)
                        part = aw[pq][:, 2 * j:2 * j + 2, :]
                        dve.tensor_tensor(part, bank[("rB", j)][:].rearrange("p (c n) -> p c n", n=N), part, ALU.mult)\
                           .then_inc(read["rB"], 1)

                def scale_hidden(js):
                    for j in js:
                        if j == 0:
                            dve.wait_ge(read["gu"], FC * fb + FC)
                        dve.wait_ge(done["cB"], 4 * fb + j + 1)
                        part = it[:, 2 * j:2 * j + 2, :]
                        dve.tensor_tensor(part, bank[("cB", j)][:].rearrange("p (c n) -> p c n", n=N), part,
                                          ALU.mult).then_inc(read["cB"], 1)

                def output_rows():
                    wait(dve, out_stored, 16 * fb)
                    for t in range(T):
                        dve.wait_ge(done["y2"], 2 * fb + t + 1)
                        dve.tensor_tensor(o_sb[:, t, :], bank[("y2", t)][:, 0:D], x1[q][:, t, :], ALU.add)\
                           .then_inc(read["y2"], 1)

                L_on, P_on = "L" in on, "P" in on
                if L_on:
                    link_l = Chain(ch_l, 3, s + 2)
                if P_on:
                    link_p = Chain(ch_p, P_OPS, s + 1)
                if O:
                    link_n = Chain(ch_n, 3, b)
                if P_on or O:
                    link_norms = Chain(ch_norms, NORM_OPS, s + 1)
                if L_on or O:
                    link_ln = Chain(ch_ln, LN_OPS, s + 2)

                def gated_heads(k):
                    if ("A" in on and k > 0) or (O and k == 0):
                        pair, ab, ap = (k - 1, s, q) if k > 0 else (NP - 1, b, pq)
                        dve.wait_ge(a2_done, 8 * ab + pair + 1)
                        dve.wait_ge(gate_ready, 4 * ab + pair // 2 + 1)
                        if pair == 0:
                            wait(dve, done["y"], 2 * (s - 1))
                        dve.tensor_tensor(aw[ap][:, pair, :], ps_a[pair % 2][:, 0:N], wt[ap][:, pair, :], ALU.mult)\
                           .then_inc(aw_done, 1)

                if at == LAST_STEP:
                    route_scores(link_f, fb)
                    gate_up([0, 1, 2])
                    route_groups(link_f)
                    gate_up([3, 4, 5])
                    route_experts(link_f, fb)
                    link_f.end()
                    gate_up([6, 7, 8])
                    scale_hidden([0, 1, 2, 3])
                    output_rows()
                    return

                for k in range(SLOTS):
                    if k == 0:
                        gated_heads(k)
                        if P_on:
                            squares(s + 1)
                            high_parts(0, s + 1)
                            for j in range(4):
                                sums(j, s + 1)
                    if k == 1:
                        if P_on:
                            sums(4, s + 1)
                        if F:
                            gate_up([0])
                        gated_heads(k)
                        if P_on:
                            sums(5, s + 1)
                        if O:
                            dve.wait_ge(done["nT"], b + 1)
                            dve.tensor_copy(n2, bank[("nT", 0)][:, 0:T * H]).then_inc(read["nT"], 1)
                        if P_on or O:
                            norms_start(link_norms, P_on, O, s)
                        if F:
                            gate_up([1, 2])
                    if k == 2:
                        for c in range(3):
                            if P_on or O:
                                newton(link_norms, nt)
                            if F:
                                gate_up([3 + c])
                            if c == 1:
                                gated_heads(k)
                        if F:
                            gate_up([6])
                        if O:
                            head_norms(link_o, b, rq2[pq])
                        if F:
                            gate_up([7])
                    if k == 3:
                        if O:
                            head_scales(link_o, b)
                            link_o.end()
                        if P_on:
                            value_scales(link_p, s + 1, rq2[pq])
                            link_p.end()
                        if F:
                            gate_up([8])
                        gated_heads(k)
                        if F and at != B:
                            route_scores(link_f, fb)
                    if k == 4:
                        if O:
                            scale_heads([0, 1, 2, 3])
                        gated_heads(k)
                        if L_on:
                            dve.wait_ge(x_loaded[q], (s + 2 - q) * 8 + 16)
                            row_stats(link_l, x_in[q], st1, mv1, 0)
                            link_l.end()
                        if F and at == B:
                            route_scores(link_f, fb)
                        if F:
                            route_groups(link_f)
                            route_experts(link_f, fb)
                            link_f.end()
                    if k == 5:
                        gated_heads(k)
                        if at == 0:
                            expert_weights()
                            dve.wait_ge(w_lo, 7)
                    if k == 6:
                        if O:
                            dve.wait_ge(x_kept, b + 1)
                            for t in range(T):
                                dve.wait_ge(done["y"], 2 * b + t + 1)
                                dve.tensor_tensor(x1[pq][:, t, :], bank[("y", t)][:, 0:D], x_res[pq][:, t, :], ALU.add)\
                                   .then_inc(read["y"], 1)
                            dve.wait_ge(read["y"], 2 * b + 2)
                            row_stats(link_n, x1[pq], st2, mv2, 1)
                            link_n.end()
                        if L_on or O:
                            seed(link_ln, ln)
                        if F:
                            scale_hidden([0, 1])
                        if L_on or O:
                            newton(link_ln, ln)
                        if F:
                            scale_hidden([2, 3])
                        if L_on or O:
                            newton(link_ln, ln)
                            newton(link_ln, ln)
                            link_ln.end()
                    if k == 7:
                        if O:
                            wait(dve, done["lg"], b)
                            normed_rows(x1[pq], mv2, 1, xn2, ln2_ready)
                        if L_on:
                            wait(dve, done["xT"], s + 2)
                            normed_rows(x_in[q], mv1, 0, xn, ln1_ready)
                        gated_heads(6)
                        gated_heads(7)
                        if at == FIRST_STEP:
                            projection_weights()
                            dve.wait_ge(w_lo, 4)
                        if P_on:
                            wait(dve, read["y"], 2 * s)
                            dve.wait_ge(x_loaded[pq], (s + 1 - pq) * 8 + 16)
                            dve.tensor_copy(x_res[pq][:], x_in[pq][:]).then_inc(x_kept, 1)
                        if O:
                            dve.wait_ge(x2h_ready, b + 1)
                            dve.tensor_tensor(x2l[:], bank[("x2T", 0)][:, 0:N], x2h[:].bitcast(F32), ALU.subtract)\
                               .then_inc(read["x2T"], 1)
                        if L_on:
                            dve.wait_ge(xh_ready, s + 3)
                            dve.tensor_tensor(xl[:], bank[("xT", 0)][:, 0:N], xh[:].bitcast(F32), ALU.subtract)\
                               .then_inc(read["xT"], 1)
                        if F:
                            output_rows()

            run_steps(dve, step)


_INS = ["L0_attn_tokens", "L0_attn_Wqg", "L0_attn_Wkv", "L0_attn_Wout", "L0_ffn_gate_kernel", "L0_ffn_gate_bias",
        "L0_ffn_w_gate", "L0_ffn_w_up", "L0_ffn_w_down", "L0_ffn_sw_gate", "L0_ffn_sw_up", "L0_ffn_sw_down"]


def kernel(**inputs):
    import numpy as np
    import concourse.bacc as bacc
    from concourse.bass_utils import run_bass_kernel_spmd

    nc = bacc.Bacc("TRN2", target_bir_lowering=False, num_devices=1)
    arrays, args = {}, []
    for name in _INS:
        a = np.ascontiguousarray(inputs[name])
        arrays[f"in_{name}"] = a
        args.append(nc.dram_tensor(f"in_{name}", a.shape, mybir.dt.from_np(a.dtype), kind="ExternalInput").ap())
    shape = inputs["L0_attn_tokens"].shape
    args.append(nc.dram_tensor("out_0", shape, F32, kind="ExternalOutput").ap())
    bass_attn_moe_layer_kernel(nc, *args)
    result = run_bass_kernel_spmd(nc, [arrays], core_ids=[0])
    return result.results[0]["out_0"]
```
